# Optimizing a Trainium2 kernel written in Bass

```python
import numpy as np
import jax
import jax.numpy as jnp

def _softmax(x, axis=-1):
    return jax.nn.softmax(x, axis=axis)

def _gelu(x):
    return jax.nn.gelu(x, approximate=True)

def _silu(x):
    return jax.nn.silu(x)

def _sigmoid(x):
    return jax.nn.sigmoid(x)

def _layernorm(x, axis=-1, eps=1e-05):
    m = jnp.mean(x, axis=axis, keepdims=True)
    v = jnp.var(x, axis=axis, keepdims=True)
    return (x - m) / jnp.sqrt(v + eps)

def _scatter_add(tgt, idx, src, axis=0):
    return tgt.at[idx].add(src)

def _segment_sum(src, seg, n):
    return jax.ops.segment_sum(src, seg, n)
kernel_name = 'mk_adj_ffn_d1_adj_r2_12a894'

def setup_inputs(seed: int=0):
    np.random.seed(seed)
    _w = jnp.asarray

    def _rec_inputs():
        import jax
        import jax.numpy as jnp
        _gk = jax.random.key(seed)
        x = -0.0005207 + 1.001 * jax.random.normal(jax.random.fold_in(_gk, 1), (4096, 128), jnp.float32)
        _a = jax.random.bernoulli(jax.random.fold_in(_gk, 2), 0.00195312, (4096, 4096))
        _af = _a.astype(jnp.float32)
        adj = _af
        return (x, adj)
    x, adj = _rec_inputs()

    def _L0_gnn_setup():
        import jax, jax.numpy as jnp
        import numpy as np
        N, M, D = (4096, 4096, 128)
        GAMMA = 0.1
        NEG = -9000000000000000.0
        XAVIER_GAIN = 1.414
        key = jax.random.key(seed)
        k1, k2, k3, k4, k5 = jax.random.split(key, 5)
        input1 = jax.random.normal(k1, (N, D), dtype=jnp.float32)
        input2 = jax.random.normal(k2, (M, D), dtype=jnp.float32)
        adj = (jax.random.uniform(k3, (N, M)) < 0.004).astype(jnp.float32)
        std = XAVIER_GAIN * float(np.sqrt(2.0 / (D + 1)))
        a1 = jax.random.normal(k4, (D, 1), dtype=jnp.float32) * std
        a2 = jax.random.normal(k5, (D, 1), dtype=jnp.float32) * std
        return {'input1': input1, 'input2': input2, 'adj': adj, 'a1': a1, 'a2': a2}
    _L0_gnn_all = _L0_gnn_setup()
    _L0_gnn_in = {k: v for k, v in _L0_gnn_all.items() if k in ('input2', 'a1', 'a2')}
    del _L0_gnn_all

    def _L0_ffn_setup():
        import jax, jax.numpy as jnp
        import numpy as np
        IN_CH = 128
        OUT_CH = 128
        key = jax.random.key(seed)
        kx, kw, kb = jax.random.split(key, 3)
        x = jax.random.normal(kx, (8, 2048, IN_CH), dtype=jnp.float32)
        bound = 1.0 / np.sqrt(IN_CH)
        weight = jax.random.uniform(kw, (OUT_CH, IN_CH), dtype=jnp.float32, minval=-bound, maxval=bound)
        bias = jax.random.uniform(kb, (OUT_CH,), dtype=jnp.float32, minval=-bound, maxval=bound)
        return {'x': x, 'weight': weight, 'bias': bias}
    _L0_ffn_all = _L0_ffn_setup()
    _L0_ffn_in = {k: v for k, v in _L0_ffn_all.items() if k in ('weight', 'bias')}
    del _L0_ffn_all
    return {'x': x, 'adj': adj, 'L0_gnn_input2': _L0_gnn_in['input2'], 'L0_gnn_a1': _L0_gnn_in['a1'], 'L0_gnn_a2': _L0_gnn_in['a2'], 'L0_ffn_weight': _L0_ffn_in['weight'], 'L0_ffn_bias': _L0_ffn_in['bias']}

def reference(x, adj, L0_gnn_input2, L0_gnn_a1, L0_gnn_a2, L0_ffn_weight, L0_ffn_bias):
    import jax
    import jax.numpy as jnp

    def _L0_gnn_ref(input1, input2, adj, a1, a2):
        import jax, jax.numpy as jnp
        import numpy as np
        N, M, D = (4096, 4096, 128)
        GAMMA = 0.1
        NEG = -9000000000000000.0
        XAVIER_GAIN = 1.414
        e = input1 @ a1 + (input2 @ a2).T
        e = jnp.where(e > 0, e, 0.2 * e)
        att = jnp.where(adj > 0, e, NEG)
        att = jax.nn.softmax(att, axis=1)
        deg = jnp.sum(adj, axis=1, keepdims=True)
        att = att * deg
        att = GAMMA * att + (1.0 - GAMMA) * adj
        return att @ input2

    def _L0_ffn_ref(x, weight, bias):
        import jax, jax.numpy as jnp
        import numpy as np
        IN_CH = 128
        OUT_CH = 128
        return jnp.einsum('bsi,oi->bso', x, weight) + bias
    x = x + _L0_gnn_ref(_layernorm(x, axis=-1), L0_gnn_input2, adj, L0_gnn_a1, L0_gnn_a2)
    x = x + _L0_ffn_ref(_layernorm(x, axis=-1)[None], L0_ffn_weight, L0_ffn_bias)[0]
    return x

_drawn_inputs = setup_inputs


def setup_inputs(seed=0):
    import zlib

    import numpy as np

    out = dict(_drawn_inputs(seed))
    spreads = {}
    factors = {'L0_ffn_bias': 3.466}
    for name, (base, spread) in spreads.items():
        noise = np.random.default_rng([zlib.crc32(name.encode()), seed]).standard_normal(out[name].shape)
        drawn = base * np.exp(spread * noise) if base else spread * noise
        out[name] = jnp.asarray(drawn.astype(out[name].dtype))
    for name, factor in factors.items():
        out[name] = (out[name] * factor).astype(out[name].dtype)
    return out
```

```python
from contextlib import ExitStack
from math import log

import concourse.bass as bass
from concourse import mybir

ALU = mybir.AluOpType
ACT = mybir.ActivationFunctionType
AX = mybir.AxisListType
F32 = mybir.dt.float32
F16 = mybir.dt.float16
BF16 = mybir.dt.bfloat16

P = 128
N, M, D = 4096, 4096, 128
TILES = 2
CHUNK = TILES * P
CHUNKS = N // CHUNK
JT = M // P
QUARTERS = 4
QJ = JT // QUARTERS
RJ = 4
SJ = QJ - RJ
WC = D + 1
EPS = 1e-5
SLOPE = 0.2
GAMMA = 0.1
WSCALE = 4096.0
LOSCALE = 2048.0
STEEP = -1e30
TINY = 1e-30
EPI = 7


def gnn_ffn(nc, x, adj, in2, a1, a2, w_t, bias, out):
    with ExitStack() as ctx:
        def sb(name, shape, dt):
            return ctx.enter_context(nc.sbuf_tensor(name, shape, dt))

        def ps(name, shape, dt):
            return ctx.enter_context(nc.psum_tensor(name, shape, dt))

        def sem(name):
            return ctx.enter_context(nc.semaphore(name))

        stage = sb("stage", [P, QUARTERS, QJ * CHUNK], F32)
        adj_b = [sb(f"adj_b{b}", [P, JT, CHUNK], BF16) for b in range(2)]
        plus = [sb(f"plus{b}", [P, JT, CHUNK], BF16) for b in range(2)]
        minus = [sb(f"minus{b}", [P, JT, CHUNK], BF16) for b in range(2)]
        steep = sb("steep", [P, 2, RJ, CHUNK], BF16)
        w_y = sb("w_y", [P, JT, 2, WC], F16)
        w_u = sb("w_u", [P, JT, 2, WC], F16)
        w_v = sb("w_v", [P, JT, 2, WC], F16)
        in2_f = plus[1][:, :, :].rearrange("p a b -> p (a b)").bitcast(F32).rearrange(
            "p (t d) -> p t d", d=D)
        scratch = minus[1][:, :, :].rearrange("p a b -> p (a b)").bitcast(F32)
        val = [scratch[:, b * QJ * WC:(b + 1) * QJ * WC].rearrange("p (t d) -> p t d", d=WC)
               for b in range(2)]
        rest = scratch[:, 2 * QJ * WC:3 * QJ * WC].rearrange("p (t d) -> p t d", d=WC)

        a1_bc = sb("a1_bc", [P, D], F32)
        a2_bc = sb("a2_bc", [P, D], F32)
        bias_bc = sb("bias_bc", [P, D], F32)
        wt_sb = sb("wt_sb", [P, D], F32)
        ident = sb("ident", [P, P], F32)
        ones = sb("ones", [P, P], F32)
        neg_half = sb("neg_half", [P, TILES], F32)
        junk = sb("junk", [P, TILES, D], F32)
        s2 = sb("s2", [P, JT], F32)
        neg_s2 = sb("neg_s2", [P, JT], F32)
        steep_s2 = sb("steep_s2", [P, JT], F32)
        s2_max = sb("s2_max", [P, 1], F32)
        top = sb("top", [P, 1], F32)
        g_col = sb("g_col", [P, 1], F32)
        bd_arg = sb("bd_arg", [P, 2, JT], F32)
        bd = sb("bd", [P, 2, JT], F32)

        x_pre = [sb(f"x_pre{b}", [P, TILES, D], F32) for b in range(2)]
        x_res = [sb(f"x_res{b}", [P, TILES, D], F32) for b in range(2)]
        pre_st = sb("pre_st", [P, TILES, 6], F32)
        pre_mv = sb("pre_mv", [P, TILES, 2], F32)
        pre_dot = [sb(f"pre_dot{b}", [P, TILES], F32) for b in range(2)]
        pre_var = sb("pre_var", [P, TILES], F32)
        pre_rstd = [sb(f"pre_rstd{b}", [P, TILES], F32) for b in range(2)]
        pre_s1 = sb("pre_s1", [P, TILES], F32)
        pre_h = sb("pre_h", [P, TILES], F32)
        ac_arg = [sb(f"ac_arg{b}", [P, 3, TILES], F32) for b in range(2)]
        ac = [sb(f"ac{b}", [P, 3, TILES], F32) for b in range(2)]
        diag = [sb(f"diag{b}", [P, CHUNK], F32) for b in range(2)]
        s1_bc = [sb(f"s1_bc{b}", [P, CHUNK], F32) for b in range(2)]

        num = [sb(f"num{t}", [P, WC], F32) for t in range(TILES)]
        num2 = [sb(f"num2_{t}", [P, WC], F32) for t in range(TILES)]
        lin = [sb(f"lin{t}", [P, D], F32) for t in range(TILES)]
        lin2 = [sb(f"lin2_{t}", [P, D], F32) for t in range(TILES)]
        zc = [sb(f"zc{t}", [P, 3], F32) for t in range(TILES)]
        x1 = [sb(f"x1_{b}", [P, TILES, D], F32) for b in range(2)]
        post_st = sb("post_st", [P, TILES, 6], F32)
        post_mv = sb("post_mv", [P, TILES, 2], F32)
        post_var = sb("post_var", [P, TILES], F32)
        post_rstd = sb("post_rstd", [P, TILES], F32)
        xn = sb("xn", [P, TILES, D], F32)
        xn_t = sb("xn_t", [P, TILES * P], F32)
        x1_bias = sb("x1_bias", [P, TILES, D], F32)
        o_buf = [sb(f"o_buf{b}", [P, TILES * D], F32) for b in range(2)]

        acc_y = [ps(f"acc_y{t}", [P, 512], F32) for t in range(TILES)]
        acc_u = [ps(f"acc_u{t}", [P, 512], F32) for t in range(TILES)]
        acc_v = [ps(f"acc_v{t}", [P, 512], F32) for t in range(TILES)]
        turned = ps("turned", [P, 512], F32)
        small = ps("small", [P, 512], F32)
        xnt_ps = turned[:, 0:CHUNK]
        s1_ps = turned[:, CHUNK:2 * CHUNK]
        ffn_ps = small[:, 0:CHUNK]
        g_ps = small[:, CHUNK:CHUNK + P]
        g_bc_ps = small[:, CHUNK + P:CHUNK + P + 1]

        in2_landed = [sem(f"in2_landed{q}") for q in range(QUARTERS)]
        a2_landed = sem("a2_landed")
        a1_landed = sem("a1_landed")
        ffn_w_landed = sem("ffn_w_landed")
        adj_landed = [sem(f"adj_landed{q}") for q in range(QUARTERS)]
        xpre_landed = [sem(f"xpre_landed{b}") for b in range(2)]
        xres_landed = [sem(f"xres_landed{b}") for b in range(2)]
        out_stored = [sem(f"out_stored{b}") for b in range(2)]
        consts_ready = sem("consts_ready")
        ident_zeroed = sem("ident_zeroed")

        waits_apart = sem("waits_apart")

        wy_high = sem("wy_high")
        wy_ready = sem("wy_ready")
        s2_ready = sem("s2_ready")
        s2_signs = sem("s2_signs")
        smax_ready = sem("smax_ready")
        smax_turned = sem("smax_turned")
        top_ready = sem("top_ready")
        top_spread = sem("top_spread")
        g_ready = sem("g_ready")
        bd_arg_ready = sem("bd_arg_ready")
        bd_ready = sem("bd_ready")
        val_ready = sem("val_ready")
        uv_high = sem("uv_high")
        rest_ready = sem("rest_ready")
        u_low = sem("u_low")
        v_low = sem("v_low")

        pre_stats = sem("pre_stats")
        pre_moments = sem("pre_moments")
        pre_pool = sem("pre_pool")
        pre_scaled = sem("pre_scaled")
        diag_ready = sem("diag_ready")
        s1_spread = sem("s1_spread")
        s1_ready = sem("s1_ready")
        ac_ready = sem("ac_ready")

        cast_done = sem("cast_done")
        steep_done = sem("steep_done")
        plus_ready = sem("plus_ready")
        minus_ready = sem("minus_ready")
        tile_done = sem("tile_done")
        num_ready = sem("num_ready")
        epi_step = sem("epi_step")
        lin_step = sem("lin_step")
        tile_left = sem("tile_left")
        post_stats = sem("post_stats")
        post_moments = sem("post_moments")
        post_pool = sem("post_pool")
        xn_ready = sem("xn_ready")
        xn_turned = sem("xn_turned")
        xnt_ready = sem("xnt_ready")
        ffn_done = sem("ffn_done")
        x1b_ready = sem("x1b_ready")
        out_ready = sem("out_ready")

        def cols(tile):
            return slice(tile * P, (tile + 1) * P)

        def run_slots(eng, slot):
            for c in range(4):
                slot(c, c % 2)
            with eng.Fori(2, CHUNKS // 2 - 1) as pair:
                slot(2 * pair, 0)
                slot(2 * pair + 1, 1)
            slot(CHUNKS - 2, 0)
            slot(CHUNKS - 1, 1)

        def inner(c):
            return not isinstance(c, int) or c >= 1

        def ahead(c, k):
            return not isinstance(c, int) or c + k < CHUNKS

        def wait_apart(eng, signal, value):
            eng.wait_ge(signal, value)
            eng.sem_inc(waits_apart)

        block = ctx.enter_context(nc.Block())

        @block.sync
        def _(sp):
            def load_adj(n, q):
                sp.dma_start(stage[:, q, :], adj[n, q]).then_inc(adj_landed[q], 16)

            sp.dma_start(a2_bc[:, :], a2.partition_broadcast(P)).then_inc(a2_landed, 16)
            for q in range(QUARTERS):
                sp.dma_start(in2_f[:, q * QJ:(q + 1) * QJ, :], in2[:, q]).then_inc(in2_landed[q], 16)
            sp.dma_start(a1_bc[:, :], a1.partition_broadcast(P)).then_inc(a1_landed, 16)
            for b in range(2):
                sp.dma_start(x_pre[b][:, :, :], x[b]).then_inc(xpre_landed[b], 16)
            for q in range(QUARTERS):
                load_adj(0, q)
            sp.dma_start(x_res[0][:, :, :], x[0]).then_inc(xres_landed[0], 16)
            sp.dma_start(wt_sb[:, :], w_t).then_inc(ffn_w_landed, 16)
            sp.dma_start(bias_bc[:, :], bias.partition_broadcast(P)).then_inc(ffn_w_landed, 16)
            for q in range(QUARTERS):
                sp.wait_ge(cast_done, q + 1)
                load_adj(1, q)

            def slot(c, b):
                if ahead(c, 2):
                    sp.wait_ge(pre_scaled, c + 1)
                    sp.dma_start(x_pre[b][:, :, :], x[c + 2]).then_inc(xpre_landed[b], 16)
                if ahead(c, 1):
                    if inner(c):
                        sp.wait_ge(tile_left, 2 * c)
                    sp.dma_start(x_res[1 - b][:, :, :], x[c + 1]).then_inc(xres_landed[1 - b], 16)
                if ahead(c, 2):
                    for q in range(QUARTERS):
                        sp.wait_ge(cast_done, 4 * c + 5 + q)
                        load_adj(c + 2, q)
                if inner(c):
                    sp.wait_ge(out_ready, c)
                    sp.dma_start(out[c - 1], o_buf[1 - b][:, :]).then_inc(out_stored[1 - b], 16)

            run_slots(sp, slot)
            last = (CHUNKS - 1) % 2
            sp.wait_ge(out_ready, CHUNKS)
            sp.dma_start(out[CHUNKS - 1], o_buf[last][:, :]).then_inc(out_stored[last], 16)
            for b in range(2):
                sp.wait_ge(out_stored[b], 16 * CHUNKS // 2)

        @block.gpsimd
        def _(pool):
            nc.gpsimd.memset(ident[:, :], 0.0).then_inc(ident_zeroed, 1)
            nc.gpsimd.memset(ones[:, :], 1.0)
            nc.gpsimd.memset(neg_half[:, :], -0.5)
            pool.wait_ge(ident_zeroed, 1)
            nc.gpsimd.affine_select(out=ident[:, :], in_=ident[:, :], compare_op=ALU.not_equal, fill=1.0,
                                    base=0, pattern=[[-1, P]], channel_multiplier=1).then_inc(consts_ready, 1)

            def scales(n, b, first):
                wait_apart(pool, pre_moments, TILES * (n + 1))
                nc.gpsimd.tensor_scalar(pre_var[:, :], pre_mv[:, :, 1], EPS, None,
                                        ALU.add).then_inc(pre_pool, 1)
                pool.wait_ge(pre_pool, 7 * n + 1)
                nc.gpsimd.tensor_tensor(pre_rstd[b][:, :], pre_var[:, :], neg_half[:, :],
                                        ALU.pow).then_inc(pre_pool, 1)
                pool.wait_ge(pre_pool, 7 * n + 2)
                pool.wait_ge(pre_scaled, n + 1)
                if not isinstance(n, int) or n >= 2:
                    pool.wait_ge(ac_ready, n - 1)
                nc.gpsimd.tensor_tensor(pre_s1[:, :], pre_dot[b][:, :], pre_rstd[b][:, :],
                                        ALU.mult).then_inc(pre_pool, 1)
                wait_apart(pool, pre_pool, 7 * n + 3)
                if first:
                    pool.wait_ge(g_ready, 1)
                nc.gpsimd.tensor_scalar(pre_h[:, :], pre_s1[:, :], g_col[:, 0:1], None,
                                        ALU.add).then_inc(pre_pool, 1)
                wait_apart(pool, pre_pool, 7 * n + 4)
                nc.gpsimd.tensor_scalar(ac_arg[b][:, 0, :], pre_h[:, :], 1.0 - SLOPE, 0.0,
                                        ALU.mult, ALU.min).then_inc(pre_pool, 1)
                nc.gpsimd.tensor_scalar(ac_arg[b][:, 2, :], pre_h[:, :], SLOPE - 1.0, 0.0,
                                        ALU.mult, ALU.min).then_inc(pre_pool, 1)
                wait_apart(pool, pre_pool, 7 * n + 6)
                nc.gpsimd.tensor_scalar(ac_arg[b][:, 1, :], ac_arg[b][:, 0, :], -log(LOSCALE), None,
                                        ALU.add).then_inc(pre_pool, 1)

            def post(n, b):
                wait_apart(pool, post_moments, TILES * (n + 1))
                nc.gpsimd.tensor_scalar(post_var[:, :], post_mv[:, :, 1], EPS, None,
                                        ALU.add).then_inc(post_pool, 1)
                pool.wait_ge(post_pool, 2 * n + 1)
                nc.gpsimd.tensor_tensor(post_rstd[:, :], post_var[:, :], neg_half[:, :],
                                        ALU.pow).then_inc(post_pool, 1)
                if not inner(n):
                    pool.wait_ge(ffn_w_landed, 32)
                else:
                    pool.wait_ge(out_ready, n)
                for t in range(TILES):
                    last_add = nc.gpsimd.tensor_tensor(x1_bias[:, t, :], x1[b][:, t, :], bias_bc[:, :], ALU.add)
                last_add.then_inc(x1b_ready, 1)

            scales(0, 0, True)
            scales(1, 1, False)

            def slot(c, b):
                if inner(c):
                    post(c - 1, 1 - b)
                if ahead(c, 2):
                    scales(c + 2, b, False)

            run_slots(pool, slot)
            post(CHUNKS - 1, (CHUNKS - 1) % 2)

        @block.scalar
        def _(act):
            def cast(n, q, b):
                act.wait_ge(adj_landed[q], 16 * (n + 1))
                nc.scalar.activation(adj_b[b][:, q * QJ:(q + 1) * QJ, :], stage[:, q, :], ACT.Copy)\
                    .then_inc(cast_done, 1)

            def sign_tests(n, q, b):
                h = q % 2
                if q >= 2 or not isinstance(n, int) or n >= 1:
                    act.wait_ge(plus_ready, 4 * n + q - 1)
                for k in range(RJ):
                    jt = q * QJ + SJ + k
                    ins = nc.scalar.activation(steep[:, h, k, :], s1_bc[b][:, :], ACT.Relu,
                                               bias=steep_s2[:, jt:jt + 1], scale=STEEP)
                ins.then_inc(steep_done, 1)

            def spread_copy(n, b):
                act.wait_ge(s1_spread, n + 1)
                if not isinstance(n, int) or n >= 3:
                    act.wait_ge(xn_turned, n - 2)
                if not isinstance(n, int) or n >= 2:
                    act.wait_ge(minus_ready, 4 * n - 4)
                nc.scalar.activation(s1_bc[b][:, :], s1_ps, ACT.Copy).then_inc(s1_ready, 1)

            def exps(n, b):
                act.wait_ge(pre_pool, 7 * (n + 1))
                if not isinstance(n, int) or n >= 2:
                    act.wait_ge(tile_left, 2 * n - 2)
                nc.scalar.activation(ac[b][:, :, :], ac_arg[b][:, :, :], ACT.Exp).then_inc(ac_ready, 1)

            def numerator(n, t, b):
                act.wait_ge(tile_done, 2 * n + t + 1)
                act.wait_ge(ac_ready, n + 1)
                nc.scalar.activation(num[t][:, :], acc_u[t][:, 0:WC], ACT.Copy,
                                     scale=ac[b][:, 0, t:t + 1]).then_inc(num_ready, 1)

            def copy_turned(n):
                act.wait_ge(xn_turned, n + 1)
                if inner(n):
                    act.wait_ge(ffn_done, n)
                nc.scalar.activation(xn_t[:, :], xnt_ps, ACT.Copy).then_inc(xnt_ready, 1)

            for q in range(QUARTERS):
                act.wait_ge(in2_landed[q], 16)
                nc.scalar.activation(w_y[:, q * QJ:(q + 1) * QJ, 0, 0:D], in2_f[:, q * QJ:(q + 1) * QJ, :],
                                     ACT.Copy, scale=WSCALE).then_inc(wy_high, 1)
            spread_copy(0, 0)
            for q in range(2):
                cast(0, q, 0)
            act.wait_ge(bd_arg_ready, 2)
            nc.scalar.activation(bd[:, :, :], bd_arg[:, :, :], ACT.Exp).then_inc(bd_ready, 1)
            act.wait_ge(s1_ready, 1)
            act.wait_ge(s2_signs, 2)
            for q in range(QUARTERS):
                if q >= 2:
                    cast(0, q, 0)
                act.wait_ge(val_ready, 2 * q + 2)
                nc.scalar.activation(w_u[:, q * QJ:(q + 1) * QJ, 0, :], val[q % 2], ACT.Copy).then_inc(uv_high, 1)
                act.wait_ge(rest_ready, q + 1)
                nc.scalar.activation(w_u[:, q * QJ:(q + 1) * QJ, 1, :], rest, ACT.Copy,
                                     scale=LOSCALE).then_inc(u_low, 1)
            for q in range(QUARTERS):
                sign_tests(0, q, 0)
            for q in range(QUARTERS):
                act.wait_ge(val_ready, 2 * (QUARTERS + q) + 2)
                nc.scalar.activation(w_v[:, q * QJ:(q + 1) * QJ, 0, :], val[q % 2], ACT.Copy).then_inc(uv_high, 1)
            exps(0, 0)
            spread_copy(1, 1)

            def slot(c, b):
                if inner(c):
                    numerator(c - 1, 1, 1 - b)
                if ahead(c, 1):
                    act.wait_ge(s1_ready, c + 2)
                    if not inner(c):
                        act.wait_ge(v_low, QUARTERS)
                    for q in range(QUARTERS - 1):
                        cast(c + 1, q, 1 - b)
                        sign_tests(c + 1, q, 1 - b)
                numerator(c, 0, b)
                if ahead(c, 1):
                    cast(c + 1, QUARTERS - 1, 1 - b)
                    sign_tests(c + 1, QUARTERS - 1, 1 - b)
                if ahead(c, 2):
                    spread_copy(c + 2, b)
                if inner(c):
                    copy_turned(c - 1)
                if ahead(c, 1):
                    exps(c + 1, 1 - b)

            run_slots(act, slot)
            numerator(CHUNKS - 1, 1, (CHUNKS - 1) % 2)
            copy_turned(CHUNKS - 1)

        @block.tensor
        def _(pe):
            def spread(n, b):
                pe.wait_ge(diag_ready, n + 1)
                if inner(n):
                    pe.wait_ge(s1_ready, n)
                if not isinstance(n, int) or n >= 4:
                    pe.wait_ge(xnt_ready, n - 3)
                nc.tensor.matmul(s1_ps, ones[:, :], diag[b][:, :], start=True, stop=True).then_inc(s1_spread, 1)

            def turn(n):
                pe.wait_ge(xn_ready, n + 1)
                if inner(n):
                    pe.wait_ge(xnt_ready, n)
                for t in range(TILES):
                    ins = nc.tensor.transpose(xnt_ps[:, cols(t)], xn[:, t, :], ident[:, :])
                ins.then_inc(xn_turned, 1)

            def linear(n):
                pe.wait_ge(xnt_ready, n + 1)
                if inner(n):
                    pe.wait_ge(out_ready, n)
                for t in range(TILES):
                    ins = nc.tensor.matmul(ffn_ps[:, cols(t)], xn_t[:, cols(t)], wt_sb[:, :],
                                           start=True, stop=True)
                ins.then_inc(ffn_done, 1)

            def product(acc, left, right, t, ready, c, weights):
                for q in range(QUARTERS):
                    if t == 0:
                        pe.wait_ge(ready, 4 * c + q + 1)
                        if not inner(c):
                            pe.wait_ge(weights, q + 1)
                    for jt in range(q * QJ, (q + 1) * QJ):
                        ins = nc.tensor.matmul(acc[:, 0:2 * WC], left[:, jt, cols(t)],
                                               right[:, jt, :, :].rearrange("p a b -> p (a b)"),
                                               start=(jt == 0), stop=(jt == JT - 1))
                return ins

            pe.wait_ge(consts_ready, 1)
            spread(0, 0)
            pe.wait_ge(smax_ready, 1)
            nc.tensor.transpose(g_ps[0:1, :], s2_max[:, :], ident[:, :]).then_inc(smax_turned, 1)
            pe.wait_ge(top_ready, 1)
            nc.tensor.matmul(g_bc_ps, ones[0:1, :], top[0:1, :], start=True, stop=True).then_inc(top_spread, 1)
            pe.wait_ge(ffn_w_landed, 32)

            def slot(c, b):
                def acc_free(t):
                    if inner(c):
                        pe.wait_ge(tile_left, 2 * c + t - 1)

                if inner(c):
                    for t in range(TILES):
                        acc_free(t)
                        product(acc_y[t], adj_b[b], w_y, t, cast_done, c, wy_ready)
                        product(acc_u[t], plus[b], w_u, t, plus_ready, c, u_low)
                        product(acc_v[t], minus[b], w_v, t, minus_ready, c, v_low).then_inc(tile_done, 1)
                        if t == 0:
                            if ahead(c, 2):
                                spread(c + 2, b)
                            turn(c - 1)
                    linear(c - 1)
                else:
                    for t in range(TILES):
                        product(acc_y[t], adj_b[b], w_y, t, cast_done, c, wy_ready)
                    for t in range(TILES):
                        product(acc_u[t], plus[b], w_u, t, plus_ready, c, u_low)
                    spread(1, 1)
                    for t in range(TILES):
                        product(acc_v[t], minus[b], w_v, t, minus_ready, c, v_low).then_inc(tile_done, 1)
                        if t == 0:
                            spread(2, 0)

            run_slots(pe, slot)
            turn(CHUNKS - 1)
            linear(CHUNKS - 1)

        @block.vector
        def _(dve):
            def pre_start(n, b):
                dve.wait_ge(xpre_landed[b], 16 * (n // 2 + 1) if isinstance(n, int) else 8 * (n - b) + 16)
                if inner(n):
                    dve.wait_ge(pre_pool, 7 * n)
                for t in range(TILES):
                    nc.vector.bn_stats(pre_st[:, t, :], x_pre[b][:, t, :]).then_inc(pre_stats, 1)
                wait_apart(dve, pre_stats, TILES * (n + 1))
                for t in range(TILES):
                    nc.vector.bn_aggr(pre_mv[:, t, :], pre_st[:, t, :]).then_inc(pre_moments, 1)
                if not inner(n):
                    dve.wait_ge(a1_landed, 16)
                for t in range(TILES):
                    dve.wait_ge(pre_moments, TILES * n + t + 1)
                    ins = nc.vector.scalar_tensor_tensor(
                        out=junk[:, t, :], in0=x_pre[b][:, t, :], scalar=pre_mv[:, t, 0:1], in1=a1_bc[:, :],
                        op0=ALU.subtract, op1=ALU.mult, accum_out=pre_dot[b][:, t:t + 1])
                ins.then_inc(pre_scaled, 1)

            def pre_end(n, b):
                dve.wait_ge(pre_pool, 7 * n + 2)
                dve.wait_ge(pre_scaled, n + 1)
                if not inner(n):
                    dve.wait_ge(consts_ready, 1)
                for t in range(TILES):
                    ins = nc.vector.tensor_scalar(diag[b][:, cols(t)], ident[:, :], pre_dot[b][:, t:t + 1],
                                                  pre_rstd[b][:, t:t + 1], ALU.mult, ALU.mult)
                ins.then_inc(diag_ready, 1)

            def masks(n, q, b):
                lo, mid, hi = q * QJ, q * QJ + SJ, (q + 1) * QJ
                dve.wait_ge(cast_done, 4 * n + q + 1)
                for jt in range(lo, mid):
                    nc.vector.scalar_tensor_tensor(out=plus[b][:, jt, :], in0=s1_bc[b][:, :],
                                                   scalar=neg_s2[:, jt:jt + 1], in1=adj_b[b][:, jt, :],
                                                   op0=ALU.is_gt, op1=ALU.mult)
                dve.wait_ge(steep_done, 4 * n + q + 1)
                nc.vector.tensor_tensor(plus[b][:, mid:hi, :], adj_b[b][:, mid:hi, :], steep[:, q % 2, :, :],
                                        ALU.is_gt).then_inc(plus_ready, 1)
                dve.wait_ge(plus_ready, 4 * n + q + 1)
                nc.vector.tensor_tensor(minus[b][:, lo:hi, :], adj_b[b][:, lo:hi, :], plus[b][:, lo:hi, :],
                                        ALU.subtract).then_inc(minus_ready, 1)

            def epilogue(n, t, b):
                g = 2 * n + t
                y_scale = (1.0 - GAMMA) / WSCALE
                dve.wait_ge(xres_landed[b], 16 * (n // 2 + 1) if isinstance(n, int) else 8 * (n - b) + 16)
                dve.wait_ge(num_ready, g + 1)
                nc.vector.scalar_tensor_tensor(out=num2[t][:, :], in0=acc_u[t][:, WC:2 * WC],
                                               scalar=ac[b][:, 1, t:t + 1], in1=num[t][:, :],
                                               op0=ALU.mult, op1=ALU.add).then_inc(epi_step, 1)
                nc.vector.scalar_tensor_tensor(out=lin[t][:, :], in0=acc_y[t][:, 0:D], scalar=y_scale,
                                               in1=x_res[b][:, t, :], op0=ALU.mult,
                                               op1=ALU.add).then_inc(lin_step, 1)
                dve.wait_ge(epi_step, EPI * g + 1)
                nc.vector.scalar_tensor_tensor(out=num[t][:, :], in0=acc_v[t][:, 0:WC],
                                               scalar=ac[b][:, 2, t:t + 1], in1=num2[t][:, :],
                                               op0=ALU.mult, op1=ALU.add).then_inc(epi_step, 1)
                dve.wait_ge(lin_step, 2 * g + 1)
                nc.vector.scalar_tensor_tensor(out=lin2[t][:, :], in0=acc_y[t][:, WC:WC + D], scalar=y_scale,
                                               in1=lin[t][:, :], op0=ALU.mult,
                                               op1=ALU.add).then_inc(lin_step, 1)
                dve.wait_ge(epi_step, EPI * g + 2)
                nc.vector.scalar_tensor_tensor(out=num2[t][:, :], in0=acc_v[t][:, WC:2 * WC],
                                               scalar=ac[b][:, 2, t:t + 1], in1=num[t][:, :],
                                               op0=ALU.mult, op1=ALU.add).then_inc(epi_step, 1)
                dve.wait_ge(epi_step, EPI * g + 3)
                nc.vector.tensor_scalar(zc[t][:, 0:1], num2[t][:, D:WC], TINY, None, ALU.max).then_inc(epi_step, 1)
                dve.wait_ge(epi_step, EPI * g + 4)
                nc.vector.reciprocal(zc[t][:, 1:2], zc[t][:, 0:1]).then_inc(epi_step, 1)
                dve.wait_ge(epi_step, EPI * g + 5)
                nc.vector.tensor_scalar(zc[t][:, 2:3], acc_y[t][:, D:WC], zc[t][:, 1:2], GAMMA,
                                        ALU.mult, ALU.mult).then_inc(epi_step, 1)
                dve.wait_ge(epi_step, EPI * g + 6)
                dve.wait_ge(lin_step, 2 * g + 2)
                nc.vector.scalar_tensor_tensor(out=x1[b][:, t, :], in0=num2[t][:, 0:D], scalar=zc[t][:, 2:3],
                                               in1=lin2[t][:, :], op0=ALU.mult, op1=ALU.add)\
                    .then_inc(epi_step, 1)
                dve.wait_ge(epi_step, EPI * g + 7)
                if inner(n) or t:
                    pass
                nc.vector.bn_stats(post_st[:, t, :], x1[b][:, t, :]).then_inc(tile_left, 1)

            def post_start(n):
                if inner(n):
                    wait_apart(dve, post_pool, 2 * n)
                wait_apart(dve, tile_left, 2 * n + 2)
                for t in range(TILES):
                    nc.vector.bn_aggr(post_mv[:, t, :], post_st[:, t, :]).then_inc(post_moments, 1)

            def post_end(n, b):
                dve.wait_ge(post_pool, 2 * n + 2)
                dve.wait_ge(post_moments, 2 * n + 2)
                if inner(n):
                    dve.wait_ge(xn_turned, n)
                for t in range(TILES):
                    ins = nc.vector.tensor_scalar(xn[:, t, :], x1[b][:, t, :], post_mv[:, t, 0:1],
                                                  post_rstd[:, t:t + 1], ALU.subtract, ALU.mult)
                ins.then_inc(xn_ready, 1)

            def finish(n, b):
                dve.wait_ge(ffn_done, n + 1)
                dve.wait_ge(x1b_ready, n + 1)
                if not isinstance(n, int) or n >= 2:
                    dve.wait_ge(out_stored[b], 16 * (n // 2) if isinstance(n, int) else 8 * (n - b))
                nc.vector.tensor_tensor(o_buf[b][:, :], ffn_ps, x1_bias[:, :, :].rearrange("p a b -> p (a b)"),
                                        ALU.add).then_inc(out_ready, 1)

            nc.vector.memset(w_y[:, :, 0, D:WC], 1.0)
            nc.vector.memset(w_y[:, :, 1, D:WC], 0.0)
            dve.wait_ge(a2_landed, 16)
            for q in range(QUARTERS):
                dve.wait_ge(in2_landed[q], 16)
                for jt in range(q * QJ, (q + 1) * QJ):
                    ins = nc.vector.tensor_tensor_reduce(scratch[:, jt * D:(jt + 1) * D], in2_f[:, jt, :], a2_bc[:, :], 1.0, 0.0,
                                                         ALU.mult, ALU.add, s2[:, jt:jt + 1])
            ins.then_inc(s2_ready, 1)
            pre_start(0, 0)
            dve.wait_ge(s2_ready, 1)
            nc.vector.tensor_reduce(s2_max[:, :], s2[:, :], AX.X, ALU.max).then_inc(smax_ready, 1)
            nc.vector.tensor_scalar(neg_s2[:, :], s2[:, :], -1.0, None, ALU.mult).then_inc(s2_signs, 1)
            nc.vector.tensor_scalar(steep_s2[:, :], s2[:, :], STEEP, None, ALU.mult).then_inc(s2_signs, 1)
            pre_end(0, 0)
            dve.wait_ge(smax_turned, 1)
            nc.vector.tensor_reduce(top[0:1, :], g_ps[0:1, :], AX.X, ALU.max).then_inc(top_ready, 1)
            for q in range(QUARTERS):
                qs = slice(q * QJ, (q + 1) * QJ)
                dve.wait_ge(wy_high, q + 1)
                nc.vector.scalar_tensor_tensor(out=w_y[:, qs, 1, 0:D], in0=in2_f[:, qs, :], scalar=WSCALE,
                                               in1=w_y[:, qs, 0, 0:D], op0=ALU.mult,
                                               op1=ALU.subtract).then_inc(wy_ready, 1)
                if q == 0:
                    dve.wait_ge(top_spread, 1)
                    nc.vector.tensor_copy(g_col[:, :], g_bc_ps).then_inc(g_ready, 1)
                    dve.wait_ge(g_ready, 1)
                    nc.vector.tensor_scalar(bd_arg[:, 0, :], s2[:, :], g_col[:, 0:1], None,
                                            ALU.subtract).then_inc(bd_arg_ready, 1)
                    nc.vector.tensor_scalar(bd_arg[:, 1, :], s2[:, :], g_col[:, 0:1], SLOPE,
                                            ALU.subtract, ALU.mult).then_inc(bd_arg_ready, 1)

            def value(k, q, step):
                qs = slice(q * QJ, (q + 1) * QJ)
                if step >= 2:
                    dve.wait_ge(uv_high, step - 1)
                    dve.wait_ge(rest_ready, min(step - 1, QUARTERS))
                    if step >= QUARTERS + 2:
                        dve.wait_ge(v_low, step - 1 - QUARTERS)
                v = val[q % 2]
                nc.vector.scalar_tensor_tensor(
                    out=v[:, :, 0:D], in0=in2_f[:, qs, :], scalar=WSCALE,
                    in1=bd[:, k, qs].unsqueeze(2).to_broadcast([P, QJ, D]),
                    op0=ALU.mult, op1=ALU.mult).then_inc(val_ready, 1)
                nc.vector.tensor_scalar(v[:, :, D], bd[:, k, qs], WSCALE, None, ALU.mult).then_inc(val_ready, 1)

            def remainder(k, q, step):
                qs = slice(q * QJ, (q + 1) * QJ)
                dve.wait_ge(uv_high, step + 1)
                dve.wait_ge(val_ready, 2 * step + 2)
                if k == 0:
                    if q:
                        dve.wait_ge(u_low, q)
                    nc.vector.tensor_tensor(rest, val[q % 2], w_u[:, qs, 0, :], ALU.subtract)\
                        .then_inc(rest_ready, 1)
                else:
                    nc.vector.tensor_tensor(w_v[:, qs, 1, :], val[q % 2], w_v[:, qs, 0, :], ALU.subtract)\
                        .then_inc(v_low, 1)

            dve.wait_ge(bd_ready, 1)
            value(0, 0, 0)
            for q in range(1, QUARTERS):
                value(0, q, q)
                remainder(0, q - 1, q - 1)
            remainder(0, QUARTERS - 1, QUARTERS - 1)
            dve.wait_ge(s1_ready, 1)
            dve.wait_ge(s2_signs, 2)
            for q in range(QUARTERS):
                masks(0, q, 0)
            value(1, 0, QUARTERS)
            for q in range(1, QUARTERS):
                value(1, q, QUARTERS + q)
                remainder(1, q - 1, QUARTERS + q - 1)
            remainder(1, QUARTERS - 1, 2 * QUARTERS - 1)
            pre_start(1, 1)
            pre_end(1, 1)

            def slot(c, b):
                if inner(c):
                    epilogue(c - 1, 1, 1 - b)
                    post_start(c - 1)
                if ahead(c, 2):
                    pre_start(c + 2, b)
                if ahead(c, 1):
                    dve.wait_ge(s1_ready, c + 2)
                    masks(c + 1, 0, 1 - b)
                if inner(c):
                    post_end(c - 1, 1 - b)
                if ahead(c, 2):
                    pre_end(c + 2, b)
                if ahead(c, 1):
                    masks(c + 1, 1, 1 - b)
                    masks(c + 1, 2, 1 - b)
                epilogue(c, 0, b)
                if ahead(c, 1):
                    masks(c + 1, 3, 1 - b)
                if inner(c):
                    finish(c - 1, 1 - b)

            run_slots(dve, slot)
            last = CHUNKS - 1
            epilogue(last, 1, last % 2)
            post_start(last)
            post_end(last, last % 2)
            finish(last, last % 2)


def kernel(x, adj, L0_gnn_input2, L0_gnn_a1, L0_gnn_a2, L0_ffn_weight, L0_ffn_bias):
    import numpy as np
    import concourse.bacc as bacc
    from concourse.bass_utils import run_bass_kernel_spmd

    adj_tiles = np.ascontiguousarray(
        np.asarray(adj).reshape(CHUNKS, P, TILES, P, QUARTERS, QJ).transpose(0, 4, 3, 5, 2, 1)
    ).reshape(CHUNKS, QUARTERS, P, QJ * CHUNK)
    arrays = {
        "x": np.asarray(x).reshape(CHUNKS, P, TILES, D),
        "adj": adj_tiles,
        "in2": np.asarray(L0_gnn_input2).reshape(P, QUARTERS, QJ, D),
        "a1": np.asarray(L0_gnn_a1).reshape(D),
        "a2": np.asarray(L0_gnn_a2).reshape(D),
        "w_t": np.ascontiguousarray(np.asarray(L0_ffn_weight).T),
        "bias": np.asarray(L0_ffn_bias),
    }
    nc = bacc.Bacc("TRN2", target_bir_lowering=False, num_devices=1)
    aps = [nc.dram_tensor(name, a.shape, F32, kind="ExternalInput").ap() for name, a in arrays.items()]
    out = nc.dram_tensor("out", (CHUNKS, P, TILES * D), F32, kind="ExternalOutput").ap()
    gnn_ffn(nc, *aps, out)
    got = run_bass_kernel_spmd(nc, [arrays], core_ids=[0])
    return got.results[0]["out"].reshape(N, D)
```

```python
from contextlib import ExitStack
from math import log

import concourse.bass as bass
from concourse import mybir

ALU = mybir.AluOpType
ACT = mybir.ActivationFunctionType
AX = mybir.AxisListType
F32 = mybir.dt.float32
F16 = mybir.dt.float16
BF16 = mybir.dt.bfloat16

P = 128
N, M, D = 4096, 4096, 128
TILES = 2
CHUNK = TILES * P
CHUNKS = N // CHUNK
JT = M // P
QUARTERS = 4
QJ = JT // QUARTERS
RJ = 6
SJ = QJ - RJ
WC = D + 1
EPS = 1e-5
SLOPE = 0.2
GAMMA = 0.1
WSCALE = 4096.0
LOSCALE = 2048.0
STEEP = -1e30
TINY = 1e-30
EPI = 7
PRE = 7


def gnn_ffn(nc, x, adj, in2, a1, a2, w_t, bias, s1_rows, out):
    with ExitStack() as ctx:
        def sb(name, shape, dt):
            return ctx.enter_context(nc.sbuf_tensor(name, shape, dt))

        def ps(name, shape, dt):
            return ctx.enter_context(nc.psum_tensor(name, shape, dt))

        def sem(name):
            return ctx.enter_context(nc.semaphore(name))

        stage = sb("stage", [P, QUARTERS, QJ * CHUNK], F32)
        adj_b = [sb(f"adj_b{b}", [P, JT, CHUNK], BF16) for b in range(2)]
        plus = [sb(f"plus{b}", [P, JT, CHUNK], BF16) for b in range(2)]
        minus = [sb(f"minus{b}", [P, JT, CHUNK], BF16) for b in range(2)]
        steep = sb("steep", [P, 2, RJ, CHUNK], BF16)
        w_y = sb("w_y", [P, JT, 2, WC], F16)
        w_u = sb("w_u", [P, JT, 2, WC], F16)
        w_v = sb("w_v", [P, JT, 2, WC], F16)
        in2_f = plus[1][:, :, :].rearrange("p a b -> p (a b)").bitcast(F32).rearrange(
            "p (t d) -> p t d", d=D)
        scratch = minus[1][:, :, :].rearrange("p a b -> p (a b)").bitcast(F32)
        val = [scratch[:, b * QJ * WC:(b + 1) * QJ * WC].rearrange("p (t d) -> p t d", d=WC)
               for b in range(2)]
        product_out = plus[0][:, :, :].rearrange("p a b -> p (a b)").bitcast(F32)

        a1_bc = sb("a1_bc", [P, D], F32)
        a2_bc = sb("a2_bc", [P, D], F32)
        bias_bc = sb("bias_bc", [P, D], F32)
        wt_sb = sb("wt_sb", [P, D], F32)
        ident = sb("ident", [P, P], F32)
        ones = sb("ones", [P, P], F32)
        neg_half = sb("neg_half", [P, TILES], F32)
        junk = sb("junk", [P, TILES, D], F32)
        s2 = sb("s2", [P, JT], F32)
        neg_s2 = sb("neg_s2", [P, JT], F32)
        steep_s2 = sb("steep_s2", [P, JT], F32)
        s2_max = sb("s2_max", [P, 1], F32)
        top = sb("top", [P, 1], F32)
        g_col = sb("g_col", [P, 1], F32)
        bd_arg = sb("bd_arg", [P, 2, JT], F32)
        bd = sb("bd", [P, 2, JT], F32)

        x_pre = [sb(f"x_pre{b}", [P, TILES, D], F32) for b in range(2)]
        x_res = [sb(f"x_res{b}", [P, TILES, D], F32) for b in range(2)]
        pre_st = sb("pre_st", [P, TILES, 6], F32)
        pre_mv = sb("pre_mv", [P, TILES, 2], F32)
        pre_dot = [sb(f"pre_dot{b}", [P, TILES], F32) for b in range(2)]
        pre_var = sb("pre_var", [P, TILES], F32)
        pre_rstd = [sb(f"pre_rstd{b}", [P, TILES], F32) for b in range(2)]
        pre_s1 = [sb(f"pre_s1_{b}", [P, TILES], F32) for b in range(2)]
        pre_h = sb("pre_h", [P, TILES], F32)
        ac_arg = [sb(f"ac_arg{b}", [P, 3, TILES], F32) for b in range(2)]
        ac = [sb(f"ac{b}", [P, 3, TILES], F32) for b in range(2)]
        s1_bc = [sb(f"s1_bc{b}", [P, CHUNK], F32) for b in range(2)]

        num = [sb(f"num{t}", [P, WC], F32) for t in range(TILES)]
        num2 = [sb(f"num2_{t}", [P, WC], F32) for t in range(TILES)]
        lin = [sb(f"lin{t}", [P, D], F32) for t in range(TILES)]
        lin2 = [sb(f"lin2_{t}", [P, D], F32) for t in range(TILES)]
        zc = [sb(f"zc{t}", [P, 3], F32) for t in range(TILES)]
        deg = [sb(f"deg{t}", [P, 1], F32) for t in range(TILES)]
        x1 = [sb(f"x1_{b}", [P, TILES, D], F32) for b in range(2)]
        post_st = sb("post_st", [P, TILES, 6], F32)
        post_mv = sb("post_mv", [P, TILES, 2], F32)
        post_var = sb("post_var", [P, TILES], F32)
        post_rstd = sb("post_rstd", [P, TILES], F32)
        xn = sb("xn", [P, TILES, D], F32)
        xn_t = sb("xn_t", [P, TILES * P], F32)
        x1_bias = sb("x1_bias", [P, TILES, D], F32)
        o_buf = [sb(f"o_buf{b}", [P, TILES * D], F32) for b in range(2)]

        acc_y = [ps(f"acc_y{t}", [P, 512], F32) for t in range(TILES)]
        acc_u = [ps(f"acc_u{t}", [P, 512], F32) for t in range(TILES)]
        acc_v = [ps(f"acc_v{t}", [P, 512], F32) for t in range(TILES)]
        turned = ps("turned", [P, 512], F32)
        small = ps("small", [P, 512], F32)
        xnt_ps = turned[:, 0:CHUNK]
        ffn_ps = small[:, 0:CHUNK]
        g_ps = acc_v[1][:, 0:P]
        g_bc_ps = acc_v[1][:, P:P + 1]

        in2_landed = [sem(f"in2_landed{q}") for q in range(QUARTERS)]
        a2_landed = sem("a2_landed")
        a1_landed = sem("a1_landed")
        ffn_w_landed = sem("ffn_w_landed")
        adj_landed = [sem(f"adj_landed{q}") for q in range(QUARTERS)]
        xpre_landed = [sem(f"xpre_landed{b}") for b in range(2)]
        xres_landed = [sem(f"xres_landed{b}") for b in range(2)]
        out_stored = [sem(f"out_stored{b}") for b in range(2)]
        s1_stored = [sem(f"s1_stored{b}") for b in range(2)]
        s1_landed = [sem(f"s1_landed{b}") for b in range(2)]
        consts_ready = sem("consts_ready")
        ident_zeroed = sem("ident_zeroed")

        waits_apart = sem("waits_apart")

        wy_high = sem("wy_high")
        wy_ready = sem("wy_ready")
        s2_ready = sem("s2_ready")
        s2_signs = sem("s2_signs")
        smax_ready = sem("smax_ready")
        smax_turned = sem("smax_turned")
        top_ready = sem("top_ready")
        top_spread = sem("top_spread")
        g_ready = sem("g_ready")
        bd_arg_ready = sem("bd_arg_ready")
        bd_ready = sem("bd_ready")
        val_ready = sem("val_ready")
        uv_high = sem("uv_high")
        u_low = sem("u_low")
        v_low = sem("v_low")

        pre_stats = sem("pre_stats")
        pre_moments = sem("pre_moments")
        pre_pool = sem("pre_pool")
        pre_scaled = sem("pre_scaled")
        ac_ready = sem("ac_ready")

        cast_done = sem("cast_done")
        steep_done = sem("steep_done")
        plus_ready = sem("plus_ready")
        minus_ready = sem("minus_ready")
        tile_done = sem("tile_done")
        num_ready = sem("num_ready")
        epi_step = sem("epi_step")
        y_done = sem("y_done")
        lin_step = sem("lin_step")
        y_left = sem("y_left")
        tile_left = sem("tile_left")
        post_stats = sem("post_stats")
        post_moments = sem("post_moments")
        post_pool = sem("post_pool")
        xn_ready = sem("xn_ready")
        xn_turned = sem("xn_turned")
        xnt_ready = sem("xnt_ready")
        ffn_done = sem("ffn_done")
        x1b_ready = sem("x1b_ready")
        out_ready = sem("out_ready")

        def cols(tile):
            return slice(tile * P, (tile + 1) * P)

        def run_slots(eng, slot):
            for c in range(4):
                slot(c, c % 2)
            with eng.Fori(2, CHUNKS // 2 - 1) as pair:
                slot(2 * pair, 0)
                slot(2 * pair + 1, 1)
            slot(CHUNKS - 2, 0)
            slot(CHUNKS - 1, 1)

        def landed(n, b):
            return 16 * (n // 2 + 1) if isinstance(n, int) else 8 * (n - b) + 16

        def inner(c):
            return not isinstance(c, int) or c >= 1

        def ahead(c, k):
            return not isinstance(c, int) or c + k < CHUNKS

        def wait_apart(eng, signal, value):
            eng.wait_ge(signal, value)
            eng.sem_inc(waits_apart)

        block = ctx.enter_context(nc.Block())

        @block.sync
        def _(sp):
            def load_adj(n, q):
                sp.dma_start(stage[:, q, :], adj[n, q]).then_inc(adj_landed[q], 16)

            def store_s1(n, b):
                sp.wait_ge(pre_pool, PRE * n + 3)
                sp.dma_start(s1_rows[n].rearrange("(t p) -> p t", p=P), pre_s1[b][:, :],
                             allow_slow_non_contiguous=True).then_inc(s1_stored[b], 16)

            def spread_s1(n, b):
                sp.wait_ge(s1_stored[b], landed(n, b))
                if not isinstance(n, int) or n >= 2:
                    sp.wait_ge(steep_done, 4 * n - 4)
                    sp.wait_ge(plus_ready, 4 * n - 4)
                sp.dma_start(s1_bc[b][:, :], s1_rows[n].partition_broadcast(P)).then_inc(s1_landed[b], 16)

            sp.dma_start(a2_bc[:, :], a2.partition_broadcast(P)).then_inc(a2_landed, 16)
            for q in range(QUARTERS):
                sp.dma_start(in2_f[:, q * QJ:(q + 1) * QJ, :], in2[:, q]).then_inc(in2_landed[q], 16)
            sp.dma_start(a1_bc[:, :], a1.partition_broadcast(P)).then_inc(a1_landed, 16)
            for b in range(2):
                sp.dma_start(x_pre[b][:, :, :], x[b]).then_inc(xpre_landed[b], 16)
            load_adj(0, 0)
            load_adj(0, 1)
            store_s1(0, 0)
            load_adj(0, 2)
            spread_s1(0, 0)
            load_adj(0, 3)
            sp.dma_start(x_res[0][:, :, :], x[0]).then_inc(xres_landed[0], 16)
            store_s1(1, 1)
            sp.dma_start(wt_sb[:, :], w_t).then_inc(ffn_w_landed, 16)
            sp.dma_start(bias_bc[:, :], bias.partition_broadcast(P)).then_inc(ffn_w_landed, 16)
            spread_s1(1, 1)
            for q in range(QUARTERS):
                sp.wait_ge(cast_done, q + 1)
                load_adj(1, q)

            def slot(c, b):
                if ahead(c, 2):
                    sp.wait_ge(pre_scaled, c + 1)
                    sp.dma_start(x_pre[b][:, :, :], x[c + 2]).then_inc(xpre_landed[b], 16)
                if ahead(c, 1):
                    if inner(c):
                        sp.wait_ge(y_left, 2 * c)
                    sp.dma_start(x_res[1 - b][:, :, :], x[c + 1]).then_inc(xres_landed[1 - b], 16)
                if ahead(c, 2):
                    for q in range(QUARTERS):
                        sp.wait_ge(cast_done, 4 * c + 5 + q)
                        load_adj(c + 2, q)
                        if q == 1:
                            store_s1(c + 2, b)
                        if q == 2:
                            spread_s1(c + 2, b)
                if inner(c):
                    sp.wait_ge(out_ready, c)
                    sp.dma_start(out[c - 1], o_buf[1 - b][:, :]).then_inc(out_stored[1 - b], 16)

            run_slots(sp, slot)
            last = (CHUNKS - 1) % 2
            sp.wait_ge(out_ready, CHUNKS)
            sp.dma_start(out[CHUNKS - 1], o_buf[last][:, :]).then_inc(out_stored[last], 16)
            for b in range(2):
                sp.wait_ge(out_stored[b], 16 * CHUNKS // 2)

        @block.gpsimd
        def _(pool):
            nc.gpsimd.memset(ident[:, :], 0.0).then_inc(ident_zeroed, 1)
            nc.gpsimd.memset(ones[:, :], 1.0)
            nc.gpsimd.memset(neg_half[:, :], -0.5)
            pool.wait_ge(ident_zeroed, 1)
            nc.gpsimd.affine_select(out=ident[:, :], in_=ident[:, :], compare_op=ALU.not_equal, fill=1.0,
                                    base=0, pattern=[[-1, P]], channel_multiplier=1).then_inc(consts_ready, 1)

            def scales(n, b, first):
                wait_apart(pool, pre_moments, TILES * (n + 1))
                nc.gpsimd.tensor_scalar(pre_var[:, :], pre_mv[:, :, 1], EPS, None,
                                        ALU.add).then_inc(pre_pool, 1)
                pool.wait_ge(pre_pool, PRE * n + 1)
                nc.gpsimd.tensor_tensor(pre_rstd[b][:, :], pre_var[:, :], neg_half[:, :],
                                        ALU.pow).then_inc(pre_pool, 1)
                pool.wait_ge(pre_pool, PRE * n + 2)
                pool.wait_ge(pre_scaled, n + 1)
                if not isinstance(n, int) or n >= 2:
                    pool.wait_ge(ac_ready, n - 1)
                    pool.wait_ge(s1_stored[b], landed(n, b) - 16)
                nc.gpsimd.tensor_tensor(pre_s1[b][:, :], pre_dot[b][:, :], pre_rstd[b][:, :],
                                        ALU.mult).then_inc(pre_pool, 1)
                wait_apart(pool, pre_pool, PRE * n + 3)
                if first:
                    pool.wait_ge(g_ready, 1)
                nc.gpsimd.tensor_scalar(pre_h[:, :], pre_s1[b][:, :], g_col[:, 0:1], None,
                                        ALU.add).then_inc(pre_pool, 1)
                wait_apart(pool, pre_pool, PRE * n + 4)
                nc.gpsimd.tensor_scalar(ac_arg[b][:, 0, :], pre_h[:, :], 1.0 - SLOPE, 0.0,
                                        ALU.mult, ALU.min).then_inc(pre_pool, 1)
                nc.gpsimd.tensor_scalar(ac_arg[b][:, 2, :], pre_h[:, :], SLOPE - 1.0, 0.0,
                                        ALU.mult, ALU.min).then_inc(pre_pool, 1)
                wait_apart(pool, pre_pool, PRE * n + 6)
                nc.gpsimd.tensor_scalar(ac_arg[b][:, 1, :], ac_arg[b][:, 0, :], -log(LOSCALE), None,
                                        ALU.add).then_inc(pre_pool, 1)

            def post(n, b):
                wait_apart(pool, post_moments, TILES * (n + 1))
                nc.gpsimd.tensor_scalar(post_var[:, :], post_mv[:, :, 1], EPS, None,
                                        ALU.add).then_inc(post_pool, 1)
                pool.wait_ge(post_pool, 2 * n + 1)
                nc.gpsimd.tensor_tensor(post_rstd[:, :], post_var[:, :], neg_half[:, :],
                                        ALU.pow).then_inc(post_pool, 1)
                if not inner(n):
                    pool.wait_ge(ffn_w_landed, 32)
                else:
                    pool.wait_ge(out_ready, n)
                for t in range(TILES):
                    last_add = nc.gpsimd.tensor_tensor(x1_bias[:, t, :], x1[b][:, t, :], bias_bc[:, :], ALU.add)
                last_add.then_inc(x1b_ready, 1)

            scales(0, 0, True)
            scales(1, 1, False)

            def slot(c, b):
                if inner(c):
                    post(c - 1, 1 - b)
                if ahead(c, 2):
                    scales(c + 2, b, False)

            run_slots(pool, slot)
            post(CHUNKS - 1, (CHUNKS - 1) % 2)

        @block.scalar
        def _(act):
            def cast(n, q, b):
                act.wait_ge(adj_landed[q], 16 * (n + 1))
                if not isinstance(n, int) or n >= 2:
                    act.wait_ge(y_done, 2 * n - 2)
                    act.wait_ge(minus_ready, 4 * n - 4)
                nc.scalar.activation(adj_b[b][:, q * QJ:(q + 1) * QJ, :], stage[:, q, :], ACT.Copy)\
                    .then_inc(cast_done, 1)

            def sign_tests(n, q, b):
                h = q % 2
                if q >= 2 or not isinstance(n, int) or n >= 1:
                    act.wait_ge(plus_ready, 4 * n + q - 1)
                for k in range(RJ):
                    jt = q * QJ + SJ + k
                    ins = nc.scalar.activation(steep[:, h, k, :], s1_bc[b][:, :], ACT.Relu,
                                               bias=steep_s2[:, jt:jt + 1], scale=STEEP)
                ins.then_inc(steep_done, 1)

            def exps(n, b):
                act.wait_ge(pre_pool, PRE * (n + 1))
                if not isinstance(n, int) or n >= 2:
                    act.wait_ge(tile_left, 2 * n - 2)
                nc.scalar.activation(ac[b][:, :, :], ac_arg[b][:, :, :], ACT.Exp).then_inc(ac_ready, 1)

            def numerator(n, t, b):
                act.wait_ge(tile_done, 2 * n + t + 1)
                act.wait_ge(ac_ready, n + 1)
                nc.scalar.activation(num[t][:, :], acc_u[t][:, 0:WC], ACT.Copy,
                                     scale=ac[b][:, 0, t:t + 1]).then_inc(num_ready, 1)

            def copy_turned(n):
                act.wait_ge(xn_turned, n + 1)
                if inner(n):
                    act.wait_ge(ffn_done, n)
                nc.scalar.activation(xn_t[:, :], xnt_ps, ACT.Copy).then_inc(xnt_ready, 1)

            for q in range(QUARTERS):
                act.wait_ge(in2_landed[q], 16)
                nc.scalar.activation(w_y[:, q * QJ:(q + 1) * QJ, 0, 0:D], in2_f[:, q * QJ:(q + 1) * QJ, :],
                                     ACT.Copy, scale=WSCALE).then_inc(wy_high, 1)
            act.wait_ge(bd_arg_ready, 2)
            nc.scalar.activation(bd[:, :, :], bd_arg[:, :, :], ACT.Exp).then_inc(bd_ready, 1)
            act.wait_ge(s2_signs, 2)
            for q in range(QUARTERS):
                act.wait_ge(val_ready, 2 * q + 2)
                nc.scalar.activation(w_u[:, q * QJ:(q + 1) * QJ, 0, :], val[q % 2], ACT.Copy,
                                     scale=1.0 / LOSCALE).then_inc(uv_high, 1)
                cast(0, q, 0)
            act.wait_ge(s1_landed[0], 16)
            for q in range(QUARTERS):
                sign_tests(0, q, 0)
            for q in range(QUARTERS):
                act.wait_ge(val_ready, 2 * (QUARTERS + q) + 2)
                nc.scalar.activation(w_v[:, q * QJ:(q + 1) * QJ, 0, :], val[q % 2], ACT.Copy).then_inc(uv_high, 1)
                cast(1, q, 1)
            exps(0, 0)

            def slot(c, b):
                def prepare(q):
                    if ahead(c, 1):
                        if q == 0:
                            act.wait_ge(s1_landed[1 - b], landed(c + 1, 1 - b))
                        if inner(c):
                            cast(c + 1, q, 1 - b)
                        sign_tests(c + 1, q, 1 - b)

                prepare(0)
                prepare(1)
                numerator(c, 0, b)
                prepare(2)
                if inner(c):
                    copy_turned(c - 1)
                prepare(3)
                if ahead(c, 1):
                    exps(c + 1, 1 - b)
                numerator(c, 1, b)

            run_slots(act, slot)
            copy_turned(CHUNKS - 1)

        @block.tensor
        def _(pe):
            def turn(n):
                pe.wait_ge(xn_ready, n + 1)
                if inner(n):
                    pe.wait_ge(xnt_ready, n)
                for t in range(TILES):
                    ins = nc.tensor.transpose(xnt_ps[:, cols(t)], xn[:, t, :], ident[:, :])
                ins.then_inc(xn_turned, 1)

            def linear(n):
                pe.wait_ge(xnt_ready, n + 1)
                if inner(n):
                    pe.wait_ge(out_ready, n)
                for t in range(TILES):
                    ins = nc.tensor.matmul(ffn_ps[:, cols(t)], xn_t[:, cols(t)], wt_sb[:, :],
                                           start=True, stop=True)
                ins.then_inc(ffn_done, 1)

            def product(acc, left, right, t, ready, c, weights):
                for q in range(QUARTERS):
                    if t == 0:
                        pe.wait_ge(ready, 4 * c + q + 1)
                        if not inner(c):
                            pe.wait_ge(weights, q + 1)
                    for jt in range(q * QJ, (q + 1) * QJ):
                        ins = nc.tensor.matmul(acc[:, 0:2 * WC], left[:, jt, cols(t)],
                                               right[:, jt, :, :].rearrange("p a b -> p (a b)"),
                                               start=(jt == 0), stop=(jt == JT - 1))
                return ins

            pe.wait_ge(consts_ready, 1)
            pe.wait_ge(smax_ready, 1)
            nc.tensor.transpose(g_ps[0:1, :], s2_max[:, :], ident[:, :]).then_inc(smax_turned, 1)
            pe.wait_ge(top_ready, 1)
            nc.tensor.matmul(g_bc_ps, ones[0:1, :], top[0:1, :], start=True, stop=True).then_inc(top_spread, 1)

            def y_product(n, b):
                for t in range(TILES):
                    if inner(n):
                        pe.wait_ge(y_left, 2 * n + t - 1)
                    product(acc_y[t], adj_b[b], w_y, t, cast_done, n, wy_ready).then_inc(y_done, 1)

            def u_product(n, t, b):
                if inner(n):
                    pe.wait_ge(tile_left, 2 * n + t - 1)
                else:
                    pe.wait_ge(g_ready, 1)
                product(acc_u[t], plus[b], w_u, t, plus_ready, n, u_low)

            def v_product(n, t, b):
                product(acc_v[t], minus[b], w_v, t, minus_ready, n, v_low).then_inc(tile_done, 1)

            y_product(0, 0)

            def slot(c, b):
                if inner(c):
                    u_product(c, 0, b)
                    v_product(c, 0, b)
                    if isinstance(c, int) and c == 1:
                        pe.wait_ge(ffn_w_landed, 32)
                    turn(c - 1)
                    u_product(c, 1, b)
                    v_product(c, 1, b)
                    linear(c - 1)
                    if ahead(c, 1):
                        y_product(c + 1, 1 - b)
                else:
                    for t in range(TILES):
                        u_product(0, t, 0)
                    y_product(1, 1)
                    for t in range(TILES):
                        v_product(0, t, 0)

            run_slots(pe, slot)
            turn(CHUNKS - 1)
            linear(CHUNKS - 1)

        @block.vector
        def _(dve):
            def pre_start(n, b):
                dve.wait_ge(xpre_landed[b], landed(n, b))
                if inner(n):
                    dve.wait_ge(pre_pool, PRE * n)
                for t in range(TILES):
                    nc.vector.bn_stats(pre_st[:, t, :], x_pre[b][:, t, :]).then_inc(pre_stats, 1)
                wait_apart(dve, pre_stats, TILES * (n + 1))
                for t in range(TILES):
                    nc.vector.bn_aggr(pre_mv[:, t, :], pre_st[:, t, :]).then_inc(pre_moments, 1)
                if not inner(n):
                    dve.wait_ge(a1_landed, 16)
                for t in range(TILES):
                    dve.wait_ge(pre_moments, TILES * n + t + 1)
                    ins = nc.vector.scalar_tensor_tensor(
                        out=junk[:, t, :], in0=x_pre[b][:, t, :], scalar=pre_mv[:, t, 0:1], in1=a1_bc[:, :],
                        op0=ALU.subtract, op1=ALU.mult, accum_out=pre_dot[b][:, t:t + 1])
                ins.then_inc(pre_scaled, 1)

            def masks(n, q, b):
                lo, mid, hi = q * QJ, q * QJ + SJ, (q + 1) * QJ
                dve.wait_ge(cast_done, 4 * n + q + 1)
                for jt in range(lo, mid):
                    nc.vector.scalar_tensor_tensor(out=plus[b][:, jt, :], in0=s1_bc[b][:, :],
                                                   scalar=neg_s2[:, jt:jt + 1], in1=adj_b[b][:, jt, :],
                                                   op0=ALU.is_gt, op1=ALU.mult)
                dve.wait_ge(steep_done, 4 * n + q + 1)
                nc.vector.tensor_tensor(plus[b][:, mid:hi, :], adj_b[b][:, mid:hi, :], steep[:, q % 2, :, :],
                                        ALU.is_gt).then_inc(plus_ready, 1)
                dve.wait_ge(plus_ready, 4 * n + q + 1)
                nc.vector.tensor_tensor(minus[b][:, lo:hi, :], adj_b[b][:, lo:hi, :], plus[b][:, lo:hi, :],
                                        ALU.subtract).then_inc(minus_ready, 1)

            def linear_part(n, t, b):
                g = 2 * n + t
                y_scale = (1.0 - GAMMA) / WSCALE
                if t == 0:
                    dve.wait_ge(xres_landed[b], landed(n, b))
                dve.wait_ge(y_done, g + 1)
                if inner(n):
                    dve.wait_ge(tile_left, g - 1)
                nc.vector.scalar_tensor_tensor(out=lin[t][:, :], in0=acc_y[t][:, 0:D], scalar=y_scale,
                                               in1=x_res[b][:, t, :], op0=ALU.mult,
                                               op1=ALU.add).then_inc(lin_step, 1)
                nc.vector.tensor_scalar(deg[t][:, :], acc_y[t][:, D:WC], GAMMA, None,
                                        ALU.mult).then_inc(lin_step, 1)
                dve.wait_ge(lin_step, 2 * g + 2)
                nc.vector.scalar_tensor_tensor(out=lin2[t][:, :], in0=acc_y[t][:, WC:WC + D], scalar=y_scale,
                                               in1=lin[t][:, :], op0=ALU.mult,
                                               op1=ALU.add).then_inc(y_left, 1)

            def epilogue(n, t, b):
                g = 2 * n + t

                def after(step):
                    dve.wait_ge(epi_step, EPI * g + step)

                dve.wait_ge(num_ready, g + 1)
                nc.vector.scalar_tensor_tensor(out=num2[t][:, :], in0=acc_u[t][:, WC:2 * WC],
                                               scalar=ac[b][:, 1, t:t + 1], in1=num[t][:, :],
                                               op0=ALU.mult, op1=ALU.add).then_inc(epi_step, 1)
                after(1)
                nc.vector.scalar_tensor_tensor(out=num[t][:, :], in0=acc_v[t][:, 0:WC],
                                               scalar=ac[b][:, 2, t:t + 1], in1=num2[t][:, :],
                                               op0=ALU.mult, op1=ALU.add).then_inc(epi_step, 1)
                after(2)
                nc.vector.scalar_tensor_tensor(out=num2[t][:, :], in0=acc_v[t][:, WC:2 * WC],
                                               scalar=ac[b][:, 2, t:t + 1], in1=num[t][:, :],
                                               op0=ALU.mult, op1=ALU.add).then_inc(epi_step, 1)
                after(3)
                nc.vector.tensor_scalar(zc[t][:, 0:1], num2[t][:, D:WC], TINY, None, ALU.max).then_inc(epi_step, 1)
                after(4)
                nc.vector.reciprocal(zc[t][:, 1:2], zc[t][:, 0:1]).then_inc(epi_step, 1)
                after(5)
                nc.vector.tensor_tensor(zc[t][:, 2:3], zc[t][:, 1:2], deg[t][:, :], ALU.mult).then_inc(epi_step, 1)
                after(6)
                dve.wait_ge(y_left, g + 1)
                nc.vector.scalar_tensor_tensor(out=x1[b][:, t, :], in0=num2[t][:, 0:D], scalar=zc[t][:, 2:3],
                                               in1=lin2[t][:, :], op0=ALU.mult, op1=ALU.add)\
                    .then_inc(epi_step, 1)
                after(7)
                nc.vector.bn_stats(post_st[:, t, :], x1[b][:, t, :]).then_inc(tile_left, 1)

            def post_start(n):
                if inner(n):
                    wait_apart(dve, post_pool, 2 * n)
                wait_apart(dve, tile_left, 2 * n + 2)
                for t in range(TILES):
                    nc.vector.bn_aggr(post_mv[:, t, :], post_st[:, t, :]).then_inc(post_moments, 1)

            def post_end(n, b):
                dve.wait_ge(post_pool, 2 * n + 2)
                dve.wait_ge(post_moments, 2 * n + 2)
                if inner(n):
                    dve.wait_ge(xn_turned, n)
                for t in range(TILES):
                    ins = nc.vector.tensor_scalar(xn[:, t, :], x1[b][:, t, :], post_mv[:, t, 0:1],
                                                  post_rstd[:, t:t + 1], ALU.subtract, ALU.mult)
                ins.then_inc(xn_ready, 1)

            def finish(n, b):
                dve.wait_ge(ffn_done, n + 1)
                dve.wait_ge(x1b_ready, n + 1)
                if not isinstance(n, int) or n >= 2:
                    dve.wait_ge(out_stored[b], 16 * (n // 2) if isinstance(n, int) else 8 * (n - b))
                nc.vector.tensor_tensor(o_buf[b][:, :], ffn_ps, x1_bias[:, :, :].rearrange("p a b -> p (a b)"),
                                        ALU.add).then_inc(out_ready, 1)

            nc.vector.memset(w_y[:, :, 0, D:WC], 1.0)
            nc.vector.memset(w_y[:, :, 1, D:WC], 0.0)
            def high_low_y(q):
                qs = slice(q * QJ, (q + 1) * QJ)
                dve.wait_ge(wy_high, q + 1)
                nc.vector.scalar_tensor_tensor(out=w_y[:, qs, 1, 0:D], in0=in2_f[:, qs, :], scalar=WSCALE,
                                               in1=w_y[:, qs, 0, 0:D], op0=ALU.mult,
                                               op1=ALU.subtract).then_inc(wy_ready, 1)

            dve.wait_ge(a2_landed, 16)
            for q in range(QUARTERS):
                dve.wait_ge(in2_landed[q], 16)
                for jt in range(q * QJ, (q + 1) * QJ):
                    ins = nc.vector.tensor_tensor_reduce(product_out[:, jt * D:(jt + 1) * D], in2_f[:, jt, :],
                                                         a2_bc[:, :], 1.0, 0.0, ALU.mult, ALU.add,
                                                         s2[:, jt:jt + 1])
            ins.then_inc(s2_ready, 1)
            pre_start(0, 0)
            dve.wait_ge(s2_ready, 1)
            nc.vector.tensor_reduce(s2_max[:, :], s2[:, :], AX.X, ALU.max).then_inc(smax_ready, 1)
            nc.vector.tensor_scalar(neg_s2[:, :], s2[:, :], -1.0, None, ALU.mult).then_inc(s2_signs, 1)
            nc.vector.tensor_scalar(steep_s2[:, :], s2[:, :], STEEP, None, ALU.mult).then_inc(s2_signs, 1)
            dve.wait_ge(smax_turned, 1)
            nc.vector.tensor_reduce(top[0:1, :], g_ps[0:1, :], AX.X, ALU.max).then_inc(top_ready, 1)
            high_low_y(0)
            dve.wait_ge(top_spread, 1)
            nc.vector.tensor_copy(g_col[:, :], g_bc_ps).then_inc(g_ready, 1)
            dve.wait_ge(g_ready, 1)
            nc.vector.tensor_scalar(bd_arg[:, 0, :], s2[:, :], g_col[:, 0:1], None,
                                    ALU.subtract).then_inc(bd_arg_ready, 1)
            nc.vector.tensor_scalar(bd_arg[:, 1, :], s2[:, :], g_col[:, 0:1], SLOPE,
                                    ALU.subtract, ALU.mult).then_inc(bd_arg_ready, 1)
            for q in range(1, QUARTERS):
                high_low_y(q)
            pre_start(1, 1)

            lift = [WSCALE * LOSCALE, WSCALE]

            def value(k, q, step):
                qs = slice(q * QJ, (q + 1) * QJ)
                if step >= 2:
                    dve.wait_ge(uv_high, step - 1)
                    dve.wait_ge(u_low, min(step - 1, QUARTERS))
                    if step >= QUARTERS + 2:
                        dve.wait_ge(v_low, step - 1 - QUARTERS)
                v = val[q % 2]
                nc.vector.scalar_tensor_tensor(
                    out=v[:, :, 0:D], in0=in2_f[:, qs, :], scalar=lift[k],
                    in1=bd[:, k, qs].unsqueeze(2).to_broadcast([P, QJ, D]),
                    op0=ALU.mult, op1=ALU.mult).then_inc(val_ready, 1)
                nc.vector.tensor_scalar(v[:, :, D], bd[:, k, qs], lift[k], None, ALU.mult).then_inc(val_ready, 1)

            def remainder(k, q, step):
                qs = slice(q * QJ, (q + 1) * QJ)
                dve.wait_ge(uv_high, step + 1)
                dve.wait_ge(val_ready, 2 * step + 2)
                w, low = (w_u, u_low) if k == 0 else (w_v, v_low)
                nc.vector.scalar_tensor_tensor(out=w[:, qs, 1, :], in0=w[:, qs, 0, :],
                                               scalar=-lift[k] / WSCALE, in1=val[q % 2],
                                               op0=ALU.mult, op1=ALU.add).then_inc(low, 1)

            dve.wait_ge(bd_ready, 1)
            value(0, 0, 0)
            for q in range(1, QUARTERS):
                value(0, q, q)
                remainder(0, q - 1, q - 1)
            remainder(0, QUARTERS - 1, QUARTERS - 1)
            dve.wait_ge(s1_landed[0], 16)
            dve.wait_ge(s2_signs, 2)
            for q in range(QUARTERS):
                masks(0, q, 0)
            for t in range(TILES):
                linear_part(0, t, 0)
            value(1, 0, QUARTERS)
            for q in range(1, QUARTERS):
                value(1, q, QUARTERS + q)
                remainder(1, q - 1, QUARTERS + q - 1)
            remainder(1, QUARTERS - 1, 2 * QUARTERS - 1)

            def slot(c, b):
                if inner(c):
                    for t in range(TILES):
                        linear_part(c, t, b)
                    post_end(c - 1, 1 - b)
                if ahead(c, 2):
                    pre_start(c + 2, b)
                if ahead(c, 1):
                    dve.wait_ge(s1_landed[1 - b], landed(c + 1, 1 - b))
                    masks(c + 1, 0, 1 - b)
                    masks(c + 1, 1, 1 - b)
                epilogue(c, 0, b)
                if ahead(c, 1):
                    masks(c + 1, 2, 1 - b)
                    masks(c + 1, 3, 1 - b)
                if inner(c):
                    finish(c - 1, 1 - b)
                epilogue(c, 1, b)
                post_start(c)

            run_slots(dve, slot)
            last = CHUNKS - 1
            post_end(last, last % 2)
            finish(last, last % 2)


def kernel(x, adj, L0_gnn_input2, L0_gnn_a1, L0_gnn_a2, L0_ffn_weight, L0_ffn_bias):
    import numpy as np
    import concourse.bacc as bacc
    from concourse.bass_utils import run_bass_kernel_spmd

    adj_tiles = np.ascontiguousarray(
        np.asarray(adj).reshape(CHUNKS, P, TILES, P, QUARTERS, QJ).transpose(0, 4, 3, 5, 2, 1)
    ).reshape(CHUNKS, QUARTERS, P, QJ * CHUNK)
    arrays = {
        "x": np.asarray(x).reshape(CHUNKS, P, TILES, D),
        "adj": adj_tiles,
        "in2": np.asarray(L0_gnn_input2).reshape(P, QUARTERS, QJ, D),
        "a1": np.asarray(L0_gnn_a1).reshape(D),
        "a2": np.asarray(L0_gnn_a2).reshape(D),
        "w_t": np.ascontiguousarray(np.asarray(L0_ffn_weight).T),
        "bias": np.asarray(L0_ffn_bias),
    }
    nc = bacc.Bacc("TRN2", target_bir_lowering=False, num_devices=1)
    aps = [nc.dram_tensor(name, a.shape, F32, kind="ExternalInput").ap() for name, a in arrays.items()]
    s1_rows = nc.dram_tensor("s1_rows", (CHUNKS, CHUNK), F32, kind="Internal").ap()
    out = nc.dram_tensor("out", (CHUNKS, P, TILES * D), F32, kind="ExternalOutput").ap()
    gnn_ffn(nc, *aps, s1_rows, out)
    got = run_bass_kernel_spmd(nc, [arrays], core_ids=[0])
    return got.results[0]["out"].reshape(N, D)
```

```python
from contextlib import ExitStack
from math import log

import concourse.bass as bass
from concourse import mybir

ALU = mybir.AluOpType
ACT = mybir.ActivationFunctionType
AX = mybir.AxisListType
F32 = mybir.dt.float32
F16 = mybir.dt.float16
I32 = mybir.dt.int32
BF16 = mybir.dt.bfloat16

P = 128
N, M, D = 4096, 4096, 128
TILES = 2
CHUNK = TILES * P
CHUNKS = N // CHUNK
JT = M // P
QUARTERS = 4
QJ = JT // QUARTERS
RJ = 6
RJ0 = 4
WC = D + 1
EPS = 1e-5
SLOPE = 0.2
GAMMA = 0.1
WSCALE = 4096.0
LOSCALE = 2048.0
STEEP = -1e30
TINY = 1e-6
EPI = 7
PRE = 7
S2_RANGE = 17.0
RANGE_AT = CHUNKS - 2
IN2_LIMIT = 65000.0
IN2_FLOOR = 16.0
NEG = 9e15
GEN = 31


def gnn_ffn(nc, x, adj, in2, a1, a2, w_t, bias, s1_rows, out):
    with ExitStack() as ctx:
        def sb(name, shape, dt):
            return ctx.enter_context(nc.sbuf_tensor(name, shape, dt))

        def ps(name, shape, dt):
            return ctx.enter_context(nc.psum_tensor(name, shape, dt))

        def sem(name):
            return ctx.enter_context(nc.semaphore(name))

        stage = sb("stage", [P, QUARTERS, QJ * CHUNK], F32)
        adj_b = [sb(f"adj_b{b}", [P, JT, CHUNK], BF16) for b in range(2)]
        plus = [sb(f"plus{b}", [P, JT, CHUNK], BF16) for b in range(2)]
        minus = [sb(f"minus{b}", [P, JT, CHUNK], BF16) for b in range(2)]
        steep = sb("steep", [P, 2, RJ, CHUNK], BF16)
        weights = [sb(f"weights_{k}", [P, JT * 2 * WC], F16) for k in "yuv"]
        w_y, w_u, w_v = [w[:, :].rearrange("p (t a b) -> p t a b", a=2, b=WC) for w in weights]
        in2_f = plus[1][:, :, :].rearrange("p a b -> p (a b)").bitcast(F32).rearrange(
            "p (t d) -> p t d", d=D)
        scratch = minus[1][:, :, :].rearrange("p a b -> p (a b)").bitcast(F32)
        val = [scratch[:, b * QJ * WC:(b + 1) * QJ * WC].rearrange("p (t d) -> p t d", d=WC)
               for b in range(3)]
        late = sb("late", [P, 5, TILES * D], F32)
        xn = late[:, 0, :].rearrange("p (t d) -> p t d", d=D)
        xn_t = late[:, 1, :]
        x1_bias = late[:, 2, :].rearrange("p (t d) -> p t d", d=D)
        o_buf = [late[:, 3 + b, :] for b in range(2)]
        val_v = [val[2], late[:, :, :].rearrange("p a b -> p (a b)")[:, 0:QJ * WC].rearrange(
            "p (t d) -> p t d", d=WC)]
        product_out = plus[0][:, :, :].rearrange("p a b -> p (a b)").bitcast(F32)

        a1_bc = sb("a1_bc", [P, D], F32)
        a2_bc = sb("a2_bc", [P, D], F32)
        bias_bc = sb("bias_bc", [P, D], F32)
        wt_sb = sb("wt_sb", [P, D], F32)
        ident = sb("ident", [P, P], F32)
        ones = sb("ones", [P, P], F32)
        neg_half = sb("neg_half", [P, TILES], F32)
        junk = sb("junk", [P, TILES, D], F32)
        s2 = sb("s2", [P, JT], F32)
        neg_s2 = sb("neg_s2", [P, JT], F32)
        steep_s2 = sb("steep_s2", [P, JT], F32)
        s2_max = sb("s2_max", [P, 1], F32)
        top = sb("top", [P, 1], F32)
        g_col = sb("g_col", [P, 1], F32)
        bd_arg = sb("bd_arg", [P, 2, JT], F32)
        bd = sb("bd", [P, 2, JT], F32)
        d_lifted = sb("d_lifted", [P, JT], F32)

        x_pre = [sb(f"x_pre{b}", [P, TILES, D], F32) for b in range(2)]
        x_res = [sb(f"x_res{b}", [P, TILES, D], F32) for b in range(2)]
        pre_st = sb("pre_st", [P, TILES, 6], F32)
        pre_mv = sb("pre_mv", [P, TILES, 2], F32)
        pre_dot = [sb(f"pre_dot{b}", [P, TILES], F32) for b in range(2)]
        pre_var = sb("pre_var", [P, TILES], F32)
        pre_rstd = [sb(f"pre_rstd{b}", [P, TILES], F32) for b in range(2)]
        pre_s1 = [sb(f"pre_s1_{b}", [P, TILES], F32) for b in range(2)]
        pre_h = sb("pre_h", [P, TILES], F32)
        ac_arg = [sb(f"ac_arg{b}", [P, 3, TILES], F32) for b in range(2)]
        ac = [sb(f"ac{b}", [P, 3, TILES], F32) for b in range(2)]
        s1_bc = [sb(f"s1_bc{b}", [P, CHUNK], F32) for b in range(2)]

        num = [sb(f"num{t}", [P, WC], F32) for t in range(TILES)]
        num2 = [sb(f"num2_{t}", [P, WC], F32) for t in range(TILES)]
        lin = [sb(f"lin{t}", [P, D], F32) for t in range(TILES)]
        lin2 = [sb(f"lin2_{t}", [P, D], F32) for t in range(TILES)]
        zc = [sb(f"zc{t}", [P, 3], F32) for t in range(TILES)]
        deg = [sb(f"deg{t}", [P, 1], F32) for t in range(TILES)]
        x1 = [sb(f"x1_{b}", [P, TILES, D], F32) for b in range(2)]
        post_st = sb("post_st", [P, TILES, 6], F32)
        post_mv = sb("post_mv", [P, TILES, 2], F32)
        post_var = sb("post_var", [P, TILES], F32)
        post_rstd = sb("post_rstd", [P, TILES], F32)

        in2_top = sb("in2_top", [P, QUARTERS], F32)
        range_col = sb("range_col", [P, 8], F32)
        outside = sb("outside", [1, 1], I32)

        acc_y = [ps(f"acc_y{t}", [P, 512], F32) for t in range(TILES)]
        acc_u = [ps(f"acc_u{t}", [P, 512], F32) for t in range(TILES)]
        acc_v = [ps(f"acc_v{t}", [P, 512], F32) for t in range(TILES)]
        turned = ps("turned", [P, 512], F32)
        small = ps("small", [P, 512], F32)
        xnt_ps = turned[:, 0:CHUNK]
        ffn_ps = small[:, 0:CHUNK]
        outside_ps = small[0:1, CHUNK:CHUNK + 1]

        def as_f32(buf):
            return buf[:, :, :].rearrange("p a b -> p (a b)").bitcast(F32).rearrange(
                "p (q r) -> p q r", q=2)

        halves = [as_f32(plus[0]), as_f32(plus[1])]
        gen_e = [halves[q // 2][:, q % 2, :] for q in range(QUARTERS)]
        halves_m = [as_f32(minus[0]), as_f32(minus[1])]
        gen_mask = [halves_m[q // 2][:, q % 2, :] for q in range(QUARTERS)]
        gen_in2 = weights[0][:, :].bitcast(F32).rearrange(
            "p (t d) -> p t d", d=WC)
        gen_max = weights[2][:, :].bitcast(F32)[:, 0:QUARTERS * CHUNK]
        gen_mcol = post_var

        g_ps = acc_v[1][:, 0:P]
        g_bc_ps = acc_v[1][:, P:P + 1]

        in2_landed = [sem(f"in2_landed{q}") for q in range(QUARTERS)]
        a2_landed = sem("a2_landed")
        a1_landed = sem("a1_landed")
        ffn_w_landed = sem("ffn_w_landed")
        adj_landed = [sem(f"adj_landed{q}") for q in range(QUARTERS)]
        xpre_landed = [sem(f"xpre_landed{b}") for b in range(2)]
        xres_landed = [sem(f"xres_landed{b}") for b in range(2)]
        out_stored = [sem(f"out_stored{b}") for b in range(2)]
        s1_stored = [sem(f"s1_stored{b}") for b in range(2)]
        s1_landed = [sem(f"s1_landed{b}") for b in range(2)]
        consts_ready = sem("consts_ready")
        ident_zeroed = sem("ident_zeroed")

        waits_apart = sem("waits_apart")

        range_step = sem("range_step")
        range_ops = sem("range_ops")
        outside_summed = sem("outside_summed")
        outside_ready = sem("outside_ready")
        gen_weights = sem("gen_weights")
        gen_ones = sem("gen_ones")
        gen_loaded = sem("gen_loaded")
        gen_step = sem("gen_step")
        gen_stored = sem("gen_stored")

        wy_high = sem("wy_high")
        wy_ready_pool = sem("wy_ready_pool")
        wy_ready_dve = sem("wy_ready_dve")
        s2_ready = sem("s2_ready")
        s2_signs = sem("s2_signs")
        smax_ready = sem("smax_ready")
        smax_turned = sem("smax_turned")
        top_ready = sem("top_ready")
        top_spread = sem("top_spread")
        g_ready = sem("g_ready")
        bd_arg_ready = sem("bd_arg_ready")
        bd_ready = sem("bd_ready")
        u_val = sem("u_val")
        v_val = sem("v_val")
        y_val = sem("y_val")
        lifted = sem("lifted")
        u_high = sem("u_high")
        v_high = sem("v_high")
        u_low = sem("u_low")
        v_low = sem("v_low")

        pre_stats = sem("pre_stats")
        pre_moments = sem("pre_moments")
        pre_pool = sem("pre_pool")
        pre_scaled = sem("pre_scaled")
        ac_ready = sem("ac_ready")

        cast_done = sem("cast_done")
        steep_done = sem("steep_done")
        plus_ready = sem("plus_ready")
        minus_ready = sem("minus_ready")
        u_done = sem("u_done")
        tile_done = sem("tile_done")
        num_ready = sem("num_ready")
        epi_step = sem("epi_step")
        y_done = sem("y_done")
        lin_step = sem("lin_step")
        y_left = sem("y_left")
        tile_left = sem("tile_left")
        post_stats = sem("post_stats")
        post_moments = sem("post_moments")
        post_pool = sem("post_pool")
        xn_ready = sem("xn_ready")
        xn_turned = sem("xn_turned")
        xnt_ready = sem("xnt_ready")
        ffn_done = sem("ffn_done")
        x1b_ready = sem("x1b_ready")
        out_ready = sem("out_ready")

        def cols(tile):
            return slice(tile * P, (tile + 1) * P)

        def run_slots(eng, slot):
            for c in range(4):
                slot(c, c % 2)
            with eng.Fori(2, CHUNKS // 2 - 1) as pair:
                slot(2 * pair, 0)
                slot(2 * pair + 1, 1)
            slot(CHUNKS - 2, 0)
            slot(CHUNKS - 1, 1)

        def landed(n, b):
            return 16 * (n // 2 + 1) if isinstance(n, int) else 8 * (n - b) + 16

        def inner(c):
            return not isinstance(c, int) or c >= 1

        def ahead(c, k):
            return not isinstance(c, int) or c + k < CHUNKS

        def wait_apart(eng, signal, value):
            eng.wait_ge(signal, value)
            eng.sem_inc(waits_apart)

        def range_left(eng):
            eng.wait_ge(outside_ready, 1)
            return eng.value_load(outside[0:1, 0:1], min_val=0, max_val=P)

        block = ctx.enter_context(nc.Block())

        @block.sync
        def _(sp):
            def load_adj(n, q):
                sp.dma_start(stage[:, q, :], adj[n, q]).then_inc(adj_landed[q], 16)

            def store_s1(n, b):
                sp.wait_ge(pre_pool, PRE * n + 3)
                sp.dma_start(s1_rows[n].rearrange("(t p) -> p t", p=P), pre_s1[b][:, :],
                             allow_slow_non_contiguous=True).then_inc(s1_stored[b], 16)

            def spread_s1(n, b):
                sp.wait_ge(s1_stored[b], landed(n, b))
                if not isinstance(n, int) or n >= 2:
                    sp.wait_ge(steep_done, 4 * n - 4)
                    sp.wait_ge(plus_ready, 4 * n - 4)
                sp.dma_start(s1_bc[b][:, :], s1_rows[n].partition_broadcast(P)).then_inc(s1_landed[b], 16)

            sp.dma_start(a2_bc[:, :], a2.partition_broadcast(P)).then_inc(a2_landed, 16)
            sp.dma_start(in2_f[:, 0:QJ, :], in2[:, 0]).then_inc(in2_landed[0], 16)
            sp.dma_start(a1_bc[:, :], a1.partition_broadcast(P)).then_inc(a1_landed, 16)
            for b in range(2):
                sp.dma_start(x_pre[b][:, :, :], x[b]).then_inc(xpre_landed[b], 16)
            for q in range(1, QUARTERS):
                sp.dma_start(in2_f[:, q * QJ:(q + 1) * QJ, :], in2[:, q]).then_inc(in2_landed[q], 16)
            load_adj(0, 0)
            load_adj(0, 1)
            store_s1(0, 0)
            load_adj(0, 2)
            spread_s1(0, 0)
            load_adj(0, 3)
            sp.dma_start(x_res[0][:, :, :], x[0]).then_inc(xres_landed[0], 16)
            sp.dma_start(wt_sb[:, :], w_t).then_inc(ffn_w_landed, 16)
            sp.dma_start(bias_bc[:, :], bias.partition_broadcast(P)).then_inc(ffn_w_landed, 16)
            for q in range(QUARTERS):
                sp.wait_ge(cast_done, q + 1)
                load_adj(1, q)
                if q == 1:
                    store_s1(1, 1)
                if q == 2:
                    spread_s1(1, 1)

            def slot(c, b):
                if ahead(c, 2):
                    sp.wait_ge(pre_scaled, c + 1)
                    sp.dma_start(x_pre[b][:, :, :], x[c + 2]).then_inc(xpre_landed[b], 16)
                if ahead(c, 1):
                    if inner(c):
                        sp.wait_ge(y_left, 2 * c)
                    sp.dma_start(x_res[1 - b][:, :, :], x[c + 1]).then_inc(xres_landed[1 - b], 16)
                if ahead(c, 2):
                    for q in range(QUARTERS):
                        sp.wait_ge(cast_done, 4 * c + 5 + q)
                        load_adj(c + 2, q)
                        if q == 1:
                            store_s1(c + 2, b)
                        if q == 2:
                            spread_s1(c + 2, b)
                if inner(c):
                    sp.wait_ge(out_ready, c)
                    sp.dma_start(out[c - 1], o_buf[1 - b]).then_inc(out_stored[1 - b], 16)

            run_slots(sp, slot)
            last = (CHUNKS - 1) % 2
            sp.wait_ge(out_ready, CHUNKS)
            sp.dma_start(out[CHUNKS - 1], o_buf[last]).then_inc(out_stored[last], 16)
            count = range_left(sp)
            for b in range(2):
                sp.wait_ge(out_stored[b], 16 * CHUNKS // 2)
            with sp.If(count != 0):
                sp.dma_start(gen_in2[:, :, 0:D], in2.rearrange("p q j d -> p (q j) d")).then_inc(gen_weights, 16)
                with sp.Fori(0, CHUNKS) as n:
                    for q in range(QUARTERS):
                        sp.dma_start(stage[:, q, :], adj[n, q]).then_inc(gen_loaded, 16)
                    sp.dma_start(s1_bc[0][:, :], s1_rows[n].partition_broadcast(P)).then_inc(gen_loaded, 16)
                    sp.dma_start(x_res[0][:, :, :], x[n]).then_inc(gen_loaded, 16)
                    sp.wait_ge(gen_step, GEN * n + GEN)
                    sp.dma_start(out[n], o_buf[0]).then_inc(gen_stored, 16)
                    wait_apart(sp, gen_stored, 16 * n + 16)

        @block.gpsimd
        def _(pool):
            nc.gpsimd.memset(ident[:, :], 0.0).then_inc(ident_zeroed, 1)
            nc.gpsimd.memset(ones[:, :], 1.0)
            nc.gpsimd.memset(neg_half[:, :], -0.5)
            pool.wait_ge(ident_zeroed, 1)
            nc.gpsimd.affine_select(out=ident[:, :], in_=ident[:, :], compare_op=ALU.not_equal, fill=1.0,
                                    base=0, pattern=[[-1, P]], channel_multiplier=1).then_inc(consts_ready, 1)

            def row_sums(n, b):
                wait_apart(pool, pre_moments, TILES * (n + 1))
                nc.gpsimd.tensor_scalar(pre_var[:, :], pre_mv[:, :, 1], EPS, None,
                                        ALU.add).then_inc(pre_pool, 1)
                pool.wait_ge(pre_pool, PRE * n + 1)
                nc.gpsimd.tensor_tensor(pre_rstd[b][:, :], pre_var[:, :], neg_half[:, :],
                                        ALU.pow).then_inc(pre_pool, 1)
                pool.wait_ge(pre_pool, PRE * n + 2)
                pool.wait_ge(pre_scaled, n + 1)
                if not isinstance(n, int) or n >= 2:
                    pool.wait_ge(ac_ready, n - 1)
                    pool.wait_ge(s1_stored[b], landed(n, b) - 16)
                nc.gpsimd.tensor_tensor(pre_s1[b][:, :], pre_dot[b][:, :], pre_rstd[b][:, :],
                                        ALU.mult).then_inc(pre_pool, 1)

            def factors(n, b, first):
                wait_apart(pool, pre_pool, PRE * n + 3)
                if first:
                    pool.wait_ge(g_ready, 1)
                nc.gpsimd.tensor_scalar(pre_h[:, :], pre_s1[b][:, :], g_col[:, 0:1], None,
                                        ALU.add).then_inc(pre_pool, 1)
                wait_apart(pool, pre_pool, PRE * n + 4)
                nc.gpsimd.tensor_scalar(ac_arg[b][:, 0, :], pre_h[:, :], 1.0 - SLOPE, 0.0,
                                        ALU.mult, ALU.min).then_inc(pre_pool, 1)
                nc.gpsimd.tensor_scalar(ac_arg[b][:, 2, :], pre_h[:, :], SLOPE - 1.0, 0.0,
                                        ALU.mult, ALU.min).then_inc(pre_pool, 1)
                wait_apart(pool, pre_pool, PRE * n + 6)
                nc.gpsimd.tensor_scalar(ac_arg[b][:, 1, :], ac_arg[b][:, 0, :], -log(LOSCALE), None,
                                        ALU.add).then_inc(pre_pool, 1)

            def post(n, b):
                wait_apart(pool, post_moments, TILES * (n + 1))
                nc.gpsimd.tensor_scalar(post_var[:, :], post_mv[:, :, 1], EPS, None,
                                        ALU.add).then_inc(post_pool, 1)
                pool.wait_ge(post_pool, 2 * n + 1)
                nc.gpsimd.tensor_tensor(post_rstd[:, :], post_var[:, :], neg_half[:, :],
                                        ALU.pow).then_inc(post_pool, 1)
                if not inner(n):
                    pool.wait_ge(ffn_w_landed, 32)
                else:
                    pool.wait_ge(out_ready, n)
                for t in range(TILES):
                    last_add = nc.gpsimd.tensor_tensor(x1_bias[:, t, :], x1[b][:, t, :], bias_bc[:, :], ALU.add)
                last_add.then_inc(x1b_ready, 1)

            def low_y(q):
                qs = slice(q * QJ, (q + 1) * QJ)
                pool.wait_ge(in2_landed[q], 16)
                if q:
                    pool.wait_ge(wy_ready_pool, q)
                nc.gpsimd.tensor_scalar(val[2][:, :, 0:D], in2_f[:, qs, :], WSCALE, 1.0,
                                        ALU.mult, ALU.mult).then_inc(y_val, 1)
                pool.wait_ge(wy_high, q + 1)
                pool.wait_ge(y_val, q + 1)
                nc.gpsimd.tensor_tensor(w_y[:, qs, 1, 0:D], val[2][:, :, 0:D], w_y[:, qs, 0, 0:D],
                                        ALU.subtract).then_inc(wy_ready_pool, 1)

            def value_v(q):
                qs = slice(q * QJ, (q + 1) * QJ)
                if q >= 2:
                    pool.wait_ge(v_low, q - 1)
                v = val_v[q % 2]
                nc.gpsimd.tensor_tensor(v[:, :, 0:D], in2_f[:, qs, :],
                                        d_lifted[:, qs].unsqueeze(2).to_broadcast([P, QJ, D]),
                                        ALU.mult).then_inc(v_val, 1)
                nc.gpsimd.tensor_copy(v[:, :, D], d_lifted[:, qs]).then_inc(v_val, 1)
                pool.wait_ge(v_val, 2 * q + 2)

            def low_v(q):
                qs = slice(q * QJ, (q + 1) * QJ)
                v = val_v[q % 2]
                pool.wait_ge(v_high, q + 1)
                nc.gpsimd.tensor_tensor(w_v[:, qs, 1, :], v, w_v[:, qs, 0, :], ALU.subtract).then_inc(v_low, 1)

            row_sums(0, 0)
            low_y(0)
            low_y(1)
            factors(0, 0, True)
            pool.wait_ge(bd_ready, 1)
            nc.gpsimd.tensor_scalar(d_lifted[:, :], bd[:, 1, :], WSCALE, 1.0, ALU.mult, ALU.mult)\
                .then_inc(lifted, 1)
            pool.wait_ge(lifted, 1)
            pool.wait_ge(wy_ready_pool, 2)
            value_v(0)
            value_v(1)
            low_v(0)
            row_sums(1, 1)
            factors(1, 1, False)
            for q in range(1, QUARTERS - 1):
                value_v(q + 1)
                low_v(q)
            low_v(QUARTERS - 1)

            def slot(c, b):
                if inner(c):
                    post(c - 1, 1 - b)
                if ahead(c, 2):
                    row_sums(c + 2, b)
                    factors(c + 2, b, False)

            run_slots(pool, slot)
            post(CHUNKS - 1, (CHUNKS - 1) % 2)
            with pool.If(range_left(pool) != 0):
                with pool.Fori(0, CHUNKS) as n:
                    wait_apart(pool, gen_step, GEN * n + 23)
                    nc.gpsimd.tensor_scalar(post_var[:, :], post_mv[:, :, 1], EPS, None,
                                            ALU.add).then_inc(gen_step, 1)
                    pool.wait_ge(gen_step, GEN * n + 24)
                    nc.gpsimd.tensor_tensor(post_rstd[:, :], post_var[:, :], neg_half[:, :],
                                            ALU.pow).then_inc(gen_step, 1)

        @block.scalar
        def _(act):
            def cast(n, q, b):
                act.wait_ge(adj_landed[q], 16 * (n + 1))
                if not isinstance(n, int) or n >= 2:
                    act.wait_ge(y_done, 2 * n - 2)
                    act.wait_ge(minus_ready, 4 * n - 4)
                nc.scalar.activation(adj_b[b][:, q * QJ:(q + 1) * QJ, :], stage[:, q, :], ACT.Copy)\
                    .then_inc(cast_done, 1)

            def sign_tests(n, q, b, tests=RJ):
                h = q % 2
                if q >= 2 or not isinstance(n, int) or n >= 1:
                    act.wait_ge(plus_ready, 4 * n + q - 1)
                for k in range(tests):
                    jt = (q + 1) * QJ - tests + k
                    ins = nc.scalar.activation(steep[:, h, k, :], s1_bc[b][:, :], ACT.Relu,
                                               bias=steep_s2[:, jt:jt + 1], scale=STEEP)
                ins.then_inc(steep_done, 1)

            def exps(n, b):
                act.wait_ge(pre_pool, PRE * (n + 1))
                if not isinstance(n, int) or n >= 2:
                    act.wait_ge(tile_left, 2 * n - 2)
                nc.scalar.activation(ac[b][:, :, :], ac_arg[b][:, :, :], ACT.Exp).then_inc(ac_ready, 1)

            def numerator(n, t, b):
                act.wait_ge(u_done, 2 * n + t + 1)
                act.wait_ge(ac_ready, n + 1)
                nc.scalar.activation(num[t][:, :], acc_u[t][:, 0:WC], ACT.Copy,
                                     scale=ac[b][:, 0, t:t + 1]).then_inc(num_ready, 1)

            def copy_turned(n):
                act.wait_ge(xn_turned, n + 1)
                if inner(n):
                    act.wait_ge(ffn_done, n)
                nc.scalar.activation(xn_t, xnt_ps, ACT.Copy).then_inc(xnt_ready, 1)

            for q in range(QUARTERS):
                act.wait_ge(in2_landed[q], 16)
                nc.scalar.activation(w_y[:, q * QJ:(q + 1) * QJ, 0, 0:D], in2_f[:, q * QJ:(q + 1) * QJ, :],
                                     ACT.Copy, scale=WSCALE).then_inc(wy_high, 1)
            cast(0, 0, 0)
            act.wait_ge(bd_arg_ready, 2)
            nc.scalar.activation(bd[:, :, :], bd_arg[:, :, :], ACT.Exp).then_inc(bd_ready, 1)
            cast(0, 1, 0)
            act.wait_ge(s2_signs, 2)

            def high_u(q):
                act.wait_ge(u_val, 2 * q + 2)
                nc.scalar.activation(w_u[:, q * QJ:(q + 1) * QJ, 0, :], val[q % 2], ACT.Copy,
                                     scale=1.0 / LOSCALE).then_inc(u_high, 1)

            def high_v(q):
                act.wait_ge(v_val, 2 * q + 2)
                nc.scalar.activation(w_v[:, q * QJ:(q + 1) * QJ, 0, :], val_v[q % 2], ACT.Copy).then_inc(v_high, 1)

            high_u(0)
            high_u(1)
            cast(0, 2, 0)
            high_v(0)
            high_u(2)
            act.wait_ge(s1_landed[0], 16)
            sign_tests(0, 0, 0, RJ0)
            cast(0, 3, 0)
            high_v(1)
            high_u(3)
            sign_tests(0, 1, 0, RJ0)
            cast(1, 0, 1)
            high_v(2)
            sign_tests(0, 2, 0, RJ0)
            cast(1, 1, 1)
            high_v(3)
            sign_tests(0, 3, 0, RJ0)
            exps(0, 0)
            cast(1, 2, 1)
            cast(1, 3, 1)

            def slot(c, b):
                def prepare(q):
                    if ahead(c, 1):
                        if q == 0:
                            act.wait_ge(s1_landed[1 - b], landed(c + 1, 1 - b))
                        if isinstance(c, int) and c == 1:
                            if q == 0:
                                cast(2, 0, 0)
                                cast(2, 1, 0)
                        elif inner(c):
                            cast(c + 1, q, 1 - b)
                        sign_tests(c + 1, q, 1 - b)

                order = ["first", "second", 0, 1, 2, 3] if isinstance(c, int) and c == 0 else \
                    [0, "cast", 1, "first", "second", 2, 3] if isinstance(c, int) and c == 1 else \
                    [0, 1, "first", 2, 3, "second"]
                for step in order:
                    if step == "cast":
                        cast(2, 2, 0)
                        cast(2, 3, 0)
                    elif step == "first":
                        numerator(c, 0, b)
                    elif step == "second":
                        numerator(c, 1, b)
                    else:
                        prepare(step)
                    if step == 2 and inner(c):
                        copy_turned(c - 1)
                    if step == 3 and ahead(c, 1):
                        exps(c + 1, 1 - b)

            run_slots(act, slot)
            copy_turned(CHUNKS - 1)
            with act.If(range_left(act) != 0):
                with act.Fori(0, CHUNKS) as n:
                    act.wait_ge(gen_step, GEN * n + 14)
                    for q in range(QUARTERS):
                        ins = nc.scalar.activation(gen_e[q], gen_e[q], ACT.Exp)
                    ins.then_inc(gen_step, 1)

        @block.tensor
        def _(pe):
            def turn(n):
                pe.wait_ge(xn_ready, n + 1)
                if inner(n):
                    pe.wait_ge(xnt_ready, n)
                for t in range(TILES):
                    ins = nc.tensor.transpose(xnt_ps[:, cols(t)], xn[:, t, :], ident[:, :])
                ins.then_inc(xn_turned, 1)

            def linear(n):
                pe.wait_ge(xnt_ready, n + 1)
                if inner(n):
                    pe.wait_ge(out_ready, n)
                if isinstance(n, int) and n == RANGE_AT:
                    pe.wait_ge(range_step, 5)
                    nc.tensor.matmul(outside_ps, range_col[:, 6:7], ones[:, 0:1],
                                     start=True, stop=True).then_inc(outside_summed, 1)
                for t in range(TILES):
                    ins = nc.tensor.matmul(ffn_ps[:, cols(t)], xn_t[:, cols(t)], wt_sb[:, :],
                                           start=True, stop=True)
                ins.then_inc(ffn_done, 1)

            def quarter(acc, left, right, t, q):
                for jt in range(q * QJ, (q + 1) * QJ):
                    ins = nc.tensor.matmul(acc[:, 0:2 * WC], left[:, jt, cols(t)],
                                           right[:, jt, :, :].rearrange("p a b -> p (a b)"),
                                           start=(jt == 0), stop=(jt == JT - 1))
                return ins

            def product(acc, left, right, t, ready, c):
                for q in range(QUARTERS):
                    if t == 0:
                        pe.wait_ge(ready, 4 * c + q + 1)
                    ins = quarter(acc, left, right, t, q)
                return ins

            pe.wait_ge(consts_ready, 1)
            pe.wait_ge(smax_ready, 1)
            nc.tensor.transpose(g_ps[0:1, :], s2_max[:, :], ident[:, :]).then_inc(smax_turned, 1)
            pe.wait_ge(top_ready, 1)
            nc.tensor.matmul(g_bc_ps, ones[0:1, :], top[0:1, :], start=True, stop=True).then_inc(top_spread, 1)

            def y_product(n, b):
                for t in range(TILES):
                    pe.wait_ge(y_left, 2 * n + t - 1)
                    product(acc_y[t], adj_b[b], w_y, t, cast_done, n).then_inc(y_done, 1)

            for q in range(QUARTERS):
                pe.wait_ge(cast_done, q + 1)
                if q < 2:
                    pe.wait_ge(wy_ready_pool, q + 1)
                else:
                    pe.wait_ge(wy_ready_dve, q - 1)
                for t in range(TILES):
                    ins = quarter(acc_y[t], adj_b[0], w_y, t, q)
                    if q == QUARTERS - 1:
                        ins.then_inc(y_done, 1)
            pe.wait_ge(g_ready, 1)
            for q in range(QUARTERS):
                pe.wait_ge(plus_ready, q + 1)
                pe.wait_ge(u_low, q + 1)
                for t in range(TILES):
                    ins = quarter(acc_u[t], plus[0], w_u, t, q)
                    if q == QUARTERS - 1:
                        ins.then_inc(u_done, 1)
                pe.wait_ge(minus_ready, q + 1)
                pe.wait_ge(v_low, q + 1)
                for t in range(TILES):
                    ins = quarter(acc_v[t], minus[0], w_v, t, q)
                    if q == QUARTERS - 1:
                        ins.then_inc(tile_done, 1)

            def slot(c, b):
                if isinstance(c, int) and c == 1:
                    pe.wait_ge(tile_left, 2)
                    for q in range(QUARTERS):
                        pe.wait_ge(plus_ready, 4 + q + 1)
                        for t in range(TILES):
                            ins = quarter(acc_u[t], plus[1], w_u, t, q)
                            if q == QUARTERS - 1:
                                ins.then_inc(u_done, 1)
                        pe.wait_ge(minus_ready, 4 + q + 1)
                        for t in range(TILES):
                            ins = quarter(acc_v[t], minus[1], w_v, t, q)
                            if q == QUARTERS - 1:
                                ins.then_inc(tile_done, 1)
                    pe.wait_ge(ffn_w_landed, 32)
                    turn(0)
                elif inner(c):
                    for t in range(TILES):
                        pe.wait_ge(tile_left, 2 * c + t - 1)
                        product(acc_u[t], plus[b], w_u, t, plus_ready, c).then_inc(u_done, 1)
                        if t == 1 and isinstance(c, int) and c == 2:
                            turn(c - 1)
                        product(acc_v[t], minus[b], w_v, t, minus_ready, c).then_inc(tile_done, 1)
                        if t == 0 and not (isinstance(c, int) and c == 2):
                            turn(c - 1)
                    linear(c - 1)
                if ahead(c, 1):
                    y_product(c + 1, 1 - b)
                if isinstance(c, int) and c == 1:
                    linear(0)

            run_slots(pe, slot)
            turn(CHUNKS - 1)
            linear(CHUNKS - 1)
            with pe.If(range_left(pe) != 0):
                pe.wait_ge(gen_ones, 1)
                with pe.Fori(0, CHUNKS) as n:
                    pe.wait_ge(gen_step, GEN * n + 8)
                    for t in range(TILES):
                        ins = nc.tensor.transpose(turned[:, cols(t)], gen_max[:, cols(t)], ident[:, :])
                    ins.then_inc(gen_step, 1)
                    pe.wait_ge(gen_step, GEN * n + 11)
                    nc.tensor.matmul(small[:, 0:CHUNK], ones[:, :], late[:, 0, :],
                                     start=True, stop=True).then_inc(gen_step, 1)
                    pe.wait_ge(gen_step, GEN * n + 15)
                    for acc, left in ((acc_u, gen_e), (acc_y, [stage[:, q, :] for q in range(QUARTERS)])):
                        for t in range(TILES):
                            for jt in range(JT):
                                k = (jt % QJ) * CHUNK + t * P
                                ins = nc.tensor.matmul(acc[t][:, 0:WC], left[jt // QJ][:, k:k + P],
                                                       gen_in2[:, jt, :], start=(jt == 0), stop=(jt == JT - 1))
                    ins.then_inc(gen_step, 1)
                    pe.wait_ge(gen_step, GEN * n + 26)
                    for t in range(TILES):
                        ins = nc.tensor.transpose(xnt_ps[:, cols(t)], xn[:, t, :], ident[:, :])
                    ins.then_inc(gen_step, 1)
                    pe.wait_ge(gen_step, GEN * n + 28)
                    for t in range(TILES):
                        ins = nc.tensor.matmul(ffn_ps[:, cols(t)], xn_t[:, cols(t)], wt_sb[:, :],
                                               start=True, stop=True)
                    ins.then_inc(gen_step, 1)

        @block.vector
        def _(dve):
            def pre_start(n, b):
                dve.wait_ge(xpre_landed[b], landed(n, b))
                if inner(n):
                    dve.wait_ge(pre_pool, PRE * n)
                for t in range(TILES):
                    nc.vector.bn_stats(pre_st[:, t, :], x_pre[b][:, t, :]).then_inc(pre_stats, 1)
                wait_apart(dve, pre_stats, TILES * (n + 1))
                for t in range(TILES):
                    nc.vector.bn_aggr(pre_mv[:, t, :], pre_st[:, t, :]).then_inc(pre_moments, 1)
                if not inner(n):
                    dve.wait_ge(a1_landed, 16)
                for t in range(TILES):
                    dve.wait_ge(pre_moments, TILES * n + t + 1)
                    ins = nc.vector.scalar_tensor_tensor(
                        out=junk[:, t, :], in0=x_pre[b][:, t, :], scalar=pre_mv[:, t, 0:1], in1=a1_bc[:, :],
                        op0=ALU.subtract, op1=ALU.mult, accum_out=pre_dot[b][:, t:t + 1])
                ins.then_inc(pre_scaled, 1)

            def compare(n, q, b, tests=RJ):
                dve.wait_ge(cast_done, 4 * n + q + 1)
                for jt in range(q * QJ, (q + 1) * QJ - tests):
                    nc.vector.scalar_tensor_tensor(out=plus[b][:, jt, :], in0=s1_bc[b][:, :],
                                                   scalar=neg_s2[:, jt:jt + 1], in1=adj_b[b][:, jt, :],
                                                   op0=ALU.is_gt, op1=ALU.mult)

            def combine(n, q, b, tests=RJ):
                lo, mid, hi = q * QJ, (q + 1) * QJ - tests, (q + 1) * QJ
                dve.wait_ge(steep_done, 4 * n + q + 1)
                nc.vector.tensor_tensor(plus[b][:, mid:hi, :], adj_b[b][:, mid:hi, :], steep[:, q % 2, 0:tests, :],
                                        ALU.is_gt).then_inc(plus_ready, 1)
                dve.wait_ge(plus_ready, 4 * n + q + 1)
                nc.vector.tensor_tensor(minus[b][:, lo:hi, :], adj_b[b][:, lo:hi, :], plus[b][:, lo:hi, :],
                                        ALU.subtract).then_inc(minus_ready, 1)

            def masks(n, q, b):
                compare(n, q, b)
                combine(n, q, b)

            def linear_part(n, t, b):
                g = 2 * n + t
                y_scale = (1.0 - GAMMA) / WSCALE
                if t == 0:
                    dve.wait_ge(xres_landed[b], landed(n, b))
                dve.wait_ge(y_done, g + 1)
                if inner(n):
                    dve.wait_ge(tile_left, g - 1)
                nc.vector.scalar_tensor_tensor(out=lin[t][:, :], in0=acc_y[t][:, 0:D], scalar=y_scale,
                                               in1=x_res[b][:, t, :], op0=ALU.mult,
                                               op1=ALU.add).then_inc(lin_step, 1)
                nc.vector.tensor_scalar(deg[t][:, :], acc_y[t][:, D:WC], GAMMA, None,
                                        ALU.mult).then_inc(lin_step, 1)
                dve.wait_ge(lin_step, 2 * g + 2)
                nc.vector.scalar_tensor_tensor(out=lin2[t][:, :], in0=acc_y[t][:, WC:WC + D], scalar=y_scale,
                                               in1=lin[t][:, :], op0=ALU.mult,
                                               op1=ALU.add).then_inc(y_left, 1)

            def epilogue(n, t, b):
                g = 2 * n + t

                def after(step):
                    dve.wait_ge(epi_step, EPI * g + step)

                dve.wait_ge(num_ready, g + 1)
                nc.vector.scalar_tensor_tensor(out=num2[t][:, :], in0=acc_u[t][:, WC:2 * WC],
                                               scalar=ac[b][:, 1, t:t + 1], in1=num[t][:, :],
                                               op0=ALU.mult, op1=ALU.add).then_inc(epi_step, 1)
                after(1)
                dve.wait_ge(tile_done, g + 1)
                nc.vector.scalar_tensor_tensor(out=num[t][:, :], in0=acc_v[t][:, 0:WC],
                                               scalar=ac[b][:, 2, t:t + 1], in1=num2[t][:, :],
                                               op0=ALU.mult, op1=ALU.add).then_inc(epi_step, 1)
                after(2)
                nc.vector.scalar_tensor_tensor(out=num2[t][:, :], in0=acc_v[t][:, WC:2 * WC],
                                               scalar=ac[b][:, 2, t:t + 1], in1=num[t][:, :],
                                               op0=ALU.mult, op1=ALU.add).then_inc(epi_step, 1)
                after(3)
                nc.vector.tensor_scalar(zc[t][:, 0:1], num2[t][:, D:WC], TINY, None, ALU.max).then_inc(epi_step, 1)
                after(4)
                nc.vector.reciprocal(zc[t][:, 1:2], zc[t][:, 0:1]).then_inc(epi_step, 1)
                after(5)
                nc.vector.tensor_tensor(zc[t][:, 2:3], zc[t][:, 1:2], deg[t][:, :], ALU.mult).then_inc(epi_step, 1)
                after(6)
                dve.wait_ge(y_left, g + 1)
                nc.vector.scalar_tensor_tensor(out=x1[b][:, t, :], in0=num2[t][:, 0:D], scalar=zc[t][:, 2:3],
                                               in1=lin2[t][:, :], op0=ALU.mult, op1=ALU.add)\
                    .then_inc(epi_step, 1)
                after(7)
                nc.vector.bn_stats(post_st[:, t, :], x1[b][:, t, :]).then_inc(tile_left, 1)

            def post_start(n):
                if inner(n):
                    wait_apart(dve, post_pool, 2 * n)
                wait_apart(dve, tile_left, 2 * n + 2)
                for t in range(TILES):
                    nc.vector.bn_aggr(post_mv[:, t, :], post_st[:, t, :]).then_inc(post_moments, 1)

            def post_end(n, b):
                dve.wait_ge(post_pool, 2 * n + 2)
                dve.wait_ge(post_moments, 2 * n + 2)
                if inner(n):
                    dve.wait_ge(xn_turned, n)
                for t in range(TILES):
                    ins = nc.vector.tensor_scalar(xn[:, t, :], x1[b][:, t, :], post_mv[:, t, 0:1],
                                                  post_rstd[:, t:t + 1], ALU.subtract, ALU.mult)
                ins.then_inc(xn_ready, 1)

            def finish(n, b):
                dve.wait_ge(ffn_done, n + 1)
                dve.wait_ge(x1b_ready, n + 1)
                if not isinstance(n, int) or n >= 2:
                    dve.wait_ge(out_stored[b], 16 * (n // 2) if isinstance(n, int) else 8 * (n - b))
                if isinstance(n, int) and n == RANGE_AT:
                    dve.wait_ge(outside_summed, 1)
                    nc.vector.tensor_copy(outside[:, :], outside_ps).then_inc(outside_ready, 1)
                nc.vector.tensor_tensor(o_buf[b], ffn_ps, late[:, 2, :],
                                        ALU.add).then_inc(out_ready, 1)

            def range_check(q):
                nc.vector.tensor_reduce(in2_top[:, q:q + 1], w_y[:, q * QJ:(q + 1) * QJ, 0, 0:D], AX.XY, ALU.max,
                                        apply_absolute_value=True).then_inc(range_step, 1)
                if q < QUARTERS - 1:
                    return
                nc.vector.tensor_scalar(range_col[:, 0:1], g_col[:, 0:1], S2_RANGE, None, ALU.subtract)
                nc.vector.tensor_reduce(range_col[:, 1:2], s2[:, :], AX.X, ALU.min).then_inc(range_ops, 1)
                dve.wait_ge(range_step, QUARTERS)
                nc.vector.tensor_reduce(range_col[:, 2:3], in2_top[:, :], AX.X, ALU.max).then_inc(range_ops, 1)
                dve.wait_ge(range_ops, 2)
                nc.vector.tensor_tensor(range_col[:, 3:4], range_col[:, 1:2], range_col[:, 0:1], ALU.is_ge)
                nc.vector.tensor_scalar(range_col[:, 4:5], range_col[:, 2:3], IN2_LIMIT, None, ALU.is_le)
                nc.vector.tensor_scalar(range_col[:, 5:6], range_col[:, 2:3], IN2_FLOOR, None,
                                        ALU.is_ge).then_inc(range_ops, 1)
                dve.wait_ge(range_ops, 3)
                nc.vector.tensor_tensor(range_col[:, 7:8], range_col[:, 3:4], range_col[:, 4:5],
                                        ALU.mult).then_inc(range_ops, 1)
                dve.wait_ge(range_ops, 4)
                nc.vector.tensor_tensor(range_col[:, 0:1], range_col[:, 7:8], range_col[:, 5:6],
                                        ALU.mult).then_inc(range_ops, 1)
                dve.wait_ge(range_ops, 5)
                nc.vector.tensor_scalar(range_col[:, 6:7], range_col[:, 0:1], 0.0, None,
                                        ALU.is_equal).then_inc(range_step, 1)

            nc.vector.memset(w_y[:, :, 0, D:WC], 1.0)
            nc.vector.memset(w_y[:, :, 1, D:WC], 0.0)

            dve.wait_ge(a2_landed, 16)
            for q in range(QUARTERS):
                dve.wait_ge(in2_landed[q], 16)
                for jt in range(q * QJ, (q + 1) * QJ):
                    ins = nc.vector.tensor_tensor_reduce(product_out[:, jt * D:(jt + 1) * D], in2_f[:, jt, :],
                                                         a2_bc[:, :], 1.0, 0.0, ALU.mult, ALU.add,
                                                         s2[:, jt:jt + 1])
                if q == 0:
                    pre_start(0, 0)
            ins.then_inc(s2_ready, 1)
            dve.wait_ge(s2_ready, 1)
            nc.vector.tensor_reduce(s2_max[:, :], s2[:, :], AX.X, ALU.max).then_inc(smax_ready, 1)
            nc.vector.tensor_scalar(neg_s2[:, :], s2[:, :], -1.0, None, ALU.mult).then_inc(s2_signs, 1)
            nc.vector.tensor_scalar(steep_s2[:, :], s2[:, :], STEEP, None, ALU.mult).then_inc(s2_signs, 1)
            dve.wait_ge(smax_turned, 1)
            nc.vector.tensor_reduce(top[0:1, :], g_ps[0:1, :], AX.X, ALU.max).then_inc(top_ready, 1)
            dve.wait_ge(top_spread, 1)
            nc.vector.tensor_copy(g_col[:, :], g_bc_ps).then_inc(g_ready, 1)
            dve.wait_ge(g_ready, 1)
            nc.vector.tensor_scalar(bd_arg[:, 0, :], s2[:, :], g_col[:, 0:1], None,
                                    ALU.subtract).then_inc(bd_arg_ready, 1)
            nc.vector.tensor_scalar(bd_arg[:, 1, :], s2[:, :], g_col[:, 0:1], SLOPE,
                                    ALU.subtract, ALU.mult).then_inc(bd_arg_ready, 1)

            def low_y(q):
                qs = slice(q * QJ, (q + 1) * QJ)
                dve.wait_ge(wy_high, q + 1)
                nc.vector.scalar_tensor_tensor(out=w_y[:, qs, 1, 0:D], in0=in2_f[:, qs, :], scalar=WSCALE,
                                               in1=w_y[:, qs, 0, 0:D], op0=ALU.mult,
                                               op1=ALU.subtract).then_inc(wy_ready_dve, 1)

            def value_u(q):
                qs = slice(q * QJ, (q + 1) * QJ)
                if q >= 2:
                    dve.wait_ge(u_high, q - 1)
                    dve.wait_ge(u_low, q - 1)
                v = val[q % 2]
                nc.vector.scalar_tensor_tensor(
                    out=v[:, :, 0:D], in0=in2_f[:, qs, :], scalar=WSCALE * LOSCALE,
                    in1=bd[:, 0, qs].unsqueeze(2).to_broadcast([P, QJ, D]),
                    op0=ALU.mult, op1=ALU.mult).then_inc(u_val, 1)
                nc.vector.tensor_scalar(v[:, :, D], bd[:, 0, qs], WSCALE * LOSCALE, None,
                                        ALU.mult).then_inc(u_val, 1)

            def low_u(q):
                qs = slice(q * QJ, (q + 1) * QJ)
                dve.wait_ge(u_high, q + 1)
                dve.wait_ge(u_val, 2 * q + 2)
                nc.vector.scalar_tensor_tensor(out=w_u[:, qs, 1, :], in0=w_u[:, qs, 0, :], scalar=-LOSCALE,
                                               in1=val[q % 2], op0=ALU.mult, op1=ALU.add).then_inc(u_low, 1)

            low_y(2)
            dve.wait_ge(bd_ready, 1)
            value_u(0)
            value_u(1)
            pre_start(1, 1)
            dve.wait_ge(s1_landed[0], 16)
            dve.wait_ge(s2_signs, 2)
            low_u(0)
            value_u(2)
            low_y(3)
            low_u(1)
            compare(0, 0, 0, RJ0)
            combine(0, 0, 0, RJ0)
            value_u(3)
            low_u(2)
            compare(0, 1, 0, RJ0)
            combine(0, 1, 0, RJ0)
            low_u(3)
            for q in range(2, QUARTERS):
                compare(0, q, 0, RJ0)
                combine(0, q, 0, RJ0)
            for t in range(TILES):
                linear_part(0, t, 0)

            def slot(c, b):
                if inner(c):
                    for t in range(TILES):
                        linear_part(c, t, b)
                    post_end(c - 1, 1 - b)
                if ahead(c, 2):
                    pre_start(c + 2, b)
                if isinstance(c, int) and c == CHUNKS - 1:
                    for q in range(QUARTERS):
                        range_check(q)
                if ahead(c, 1):
                    dve.wait_ge(s1_landed[1 - b], landed(c + 1, 1 - b))
                    if not inner(c):
                        dve.wait_ge(v_low, QUARTERS)
                order = ["compare", "first", "second", "combine", 1, 2, 3] if isinstance(c, int) and c == 0 else \
                    [0, 1, "first", 2, 3, "second"]
                for step in order:
                    if step == "first":
                        epilogue(c, 0, b)
                    elif step == "second":
                        epilogue(c, 1, b)
                    elif step == "compare":
                        compare(1, 0, 1)
                    elif step == "combine":
                        combine(1, 0, 1)
                    elif ahead(c, 1):
                        masks(c + 1, step, 1 - b)
                    if step == 3 and inner(c) and ahead(c, 1):
                        finish(c - 1, 1 - b)
                post_start(c)
                if not ahead(c, 1):
                    finish(c - 1, 1 - b)

            run_slots(dve, slot)
            last = CHUNKS - 1
            post_end(last, last % 2)
            finish(last, last % 2)

            with dve.If(range_left(dve) != 0):
                dve.wait_ge(gen_weights, 16)
                nc.vector.memset(gen_in2[:, :, D:WC], 1.0).then_inc(gen_ones, 1)
                with dve.Fori(0, CHUNKS) as n:
                    quarters = range(QUARTERS)

                    def after(step):
                        dve.wait_ge(gen_step, GEN * n + step)

                    dve.wait_ge(gen_loaded, 16 * 6 * n + 16 * 6)
                    for jt in range(JT):
                        k = (jt % QJ) * CHUNK
                        ins = nc.vector.tensor_scalar(gen_e[jt // QJ][:, k:k + CHUNK], s1_bc[0][:, :],
                                                      s2[:, jt:jt + 1], None, ALU.add)
                    ins.then_inc(gen_step, 1)
                    after(1)
                    for q in quarters:
                        ins = nc.vector.scalar_tensor_tensor(out=gen_e[q], in0=gen_e[q], scalar=SLOPE, in1=gen_e[q],
                                                             op0=ALU.mult, op1=ALU.max)
                    ins.then_inc(gen_step, 1)
                    after(2)
                    for q in quarters:
                        ins = nc.vector.tensor_tensor(gen_e[q], gen_e[q], stage[:, q, :], ALU.mult)
                    ins.then_inc(gen_step, 1)
                    after(3)
                    for q in quarters:
                        ins = nc.vector.tensor_scalar(gen_mask[q], stage[:, q, :], NEG, NEG,
                                                      ALU.mult, ALU.subtract)
                    ins.then_inc(gen_step, 1)
                    after(4)
                    for q in quarters:
                        ins = nc.vector.tensor_tensor(gen_e[q], gen_e[q], gen_mask[q], ALU.add)
                    ins.then_inc(gen_step, 1)
                    after(5)
                    for q in quarters:
                        ins = nc.vector.tensor_reduce(gen_max[:, q * CHUNK:(q + 1) * CHUNK],
                                                      gen_e[q].rearrange("p (j i) -> p i j", j=QJ), AX.X, ALU.max)
                    ins.then_inc(gen_step, 1)
                    after(6)
                    nc.vector.tensor_tensor(gen_max[:, 0:2 * CHUNK], gen_max[:, 0:2 * CHUNK],
                                            gen_max[:, 2 * CHUNK:4 * CHUNK], ALU.max).then_inc(gen_step, 1)
                    after(7)
                    nc.vector.tensor_tensor(gen_max[:, 0:CHUNK], gen_max[:, 0:CHUNK],
                                            gen_max[:, CHUNK:2 * CHUNK], ALU.max).then_inc(gen_step, 1)
                    after(9)
                    nc.vector.tensor_reduce(gen_mcol[:, :], turned[:, 0:CHUNK].rearrange("p (t j) -> p t j", j=P),
                                            AX.X, ALU.max).then_inc(gen_step, 1)
                    after(10)
                    for t in range(TILES):
                        ins = nc.vector.tensor_scalar(xn[:, t, :], ident[:, :], gen_mcol[:, t:t + 1], None, ALU.mult)
                    ins.then_inc(gen_step, 1)
                    after(12)
                    nc.vector.tensor_copy(s1_bc[1][:, :], small[:, 0:CHUNK]).then_inc(gen_step, 1)
                    after(13)
                    for q in quarters:
                        e = gen_e[q].rearrange("p (j i) -> p j i", j=QJ)
                        ins = nc.vector.tensor_tensor(e, e, s1_bc[1][:, :].unsqueeze(1).to_broadcast([P, QJ, CHUNK]),
                                                      ALU.subtract)
                    ins.then_inc(gen_step, 1)
                    after(16)
                    for t in range(TILES):
                        ins = nc.vector.reciprocal(zc[t][:, 0:1], acc_u[t][:, D:WC])
                    ins.then_inc(gen_step, 1)
                    for t in range(TILES):
                        ins = nc.vector.tensor_scalar(zc[t][:, 1:2], acc_y[t][:, D:WC], GAMMA, None, ALU.mult)
                    ins.then_inc(gen_step, 1)
                    after(18)
                    for t in range(TILES):
                        ins = nc.vector.tensor_tensor(zc[t][:, 2:3], zc[t][:, 0:1], zc[t][:, 1:2], ALU.mult)
                    ins.then_inc(gen_step, 1)
                    for t in range(TILES):
                        ins = nc.vector.scalar_tensor_tensor(out=lin[t][:, :], in0=acc_y[t][:, 0:D],
                                                             scalar=1.0 - GAMMA, in1=x_res[0][:, t, :],
                                                             op0=ALU.mult, op1=ALU.add)
                    ins.then_inc(gen_step, 1)
                    after(20)
                    for t in range(TILES):
                        ins = nc.vector.scalar_tensor_tensor(out=x1[0][:, t, :], in0=acc_u[t][:, 0:D],
                                                             scalar=zc[t][:, 2:3], in1=lin[t][:, :],
                                                             op0=ALU.mult, op1=ALU.add)
                    ins.then_inc(gen_step, 1)
                    after(21)
                    for t in range(TILES):
                        ins = nc.vector.bn_stats(post_st[:, t, :], x1[0][:, t, :])
                    ins.then_inc(gen_step, 1)
                    wait_apart(dve, gen_step, GEN * n + 22)
                    for t in range(TILES):
                        ins = nc.vector.bn_aggr(post_mv[:, t, :], post_st[:, t, :])
                    ins.then_inc(gen_step, 1)
                    after(25)
                    for t in range(TILES):
                        ins = nc.vector.tensor_scalar(xn[:, t, :], x1[0][:, t, :], post_mv[:, t, 0:1],
                                                      post_rstd[:, t:t + 1], ALU.subtract, ALU.mult)
                    ins.then_inc(gen_step, 1)
                    after(27)
                    nc.vector.tensor_copy(xn_t, xnt_ps).then_inc(gen_step, 1)
                    after(29)
                    for t in range(TILES):
                        ins = nc.vector.tensor_tensor(x1_bias[:, t, :], x1[0][:, t, :], bias_bc[:, :], ALU.add)
                    ins.then_inc(gen_step, 1)
                    after(30)
                    nc.vector.tensor_tensor(o_buf[0], ffn_ps, late[:, 2, :],
                                            ALU.add).then_inc(gen_step, 1)


def kernel(x, adj, L0_gnn_input2, L0_gnn_a1, L0_gnn_a2, L0_ffn_weight, L0_ffn_bias):
    import numpy as np
    import concourse.bacc as bacc
    from concourse.bass_utils import run_bass_kernel_spmd

    adj_tiles = np.ascontiguousarray(
        np.asarray(adj).reshape(CHUNKS, P, TILES, P, QUARTERS, QJ).transpose(0, 4, 3, 5, 2, 1)
    ).reshape(CHUNKS, QUARTERS, P, QJ * CHUNK)
    arrays = {
        "x": np.asarray(x).reshape(CHUNKS, P, TILES, D),
        "adj": adj_tiles,
        "in2": np.asarray(L0_gnn_input2).reshape(P, QUARTERS, QJ, D),
        "a1": np.asarray(L0_gnn_a1).reshape(D),
        "a2": np.asarray(L0_gnn_a2).reshape(D),
        "w_t": np.ascontiguousarray(np.asarray(L0_ffn_weight).T),
        "bias": np.asarray(L0_ffn_bias),
    }
    nc = bacc.Bacc("TRN2", target_bir_lowering=False, num_devices=1)
    aps = [nc.dram_tensor(name, a.shape, F32, kind="ExternalInput").ap() for name, a in arrays.items()]
    s1_rows = nc.dram_tensor("s1_rows", (CHUNKS, CHUNK), F32, kind="Internal").ap()
    out = nc.dram_tensor("out", (CHUNKS, P, TILES * D), F32, kind="ExternalOutput").ap()
    gnn_ffn(nc, *aps, s1_rows, out)
    got = run_bass_kernel_spmd(nc, [arrays], core_ids=[0])
    return got.results[0]["out"].reshape(N, D)
```
